# Optimizing a Trainium2 kernel written in Bass

```python
import numpy as np
import jax
import jax.numpy as jnp

def _softmax(x, axis=-1):
    return jax.nn.softmax(x, axis=axis)

def _gelu(x):
    return jax.nn.gelu(x, approximate=True)

def _silu(x):
    return jax.nn.silu(x)

def _sigmoid(x):
    return jax.nn.sigmoid(x)

def _layernorm(x, axis=-1, eps=1e-05):
    m = jnp.mean(x, axis=axis, keepdims=True)
    v = jnp.var(x, axis=axis, keepdims=True)
    return (x - m) / jnp.sqrt(v + eps)

def _scatter_add(tgt, idx, src, axis=0):
    return tgt.at[idx].add(src)

def _segment_sum(src, seg, n):
    return jax.ops.segment_sum(src, seg, n)
kernel_name = 'mk_gnn_preln_d1_gnn_r32_9c816e'

def setup_inputs(seed: int=0):
    np.random.seed(seed)
    _w = jnp.asarray

    def _rec_inputs():
        import jax
        import jax.numpy as jnp
        _gk = jax.random.key(seed)
        x = -0.0003713 + 1 * jax.random.normal(jax.random.fold_in(_gk, 1), (3125, 128), jnp.float32)
        _s = jax.random.randint(jax.random.fold_in(_gk, 2), (50000,), 0, 3125, jnp.int32)
        _d = jax.random.randint(jax.random.fold_in(_gk, 3), (50000,), 0, 3125, jnp.int32)
        _loop = jnp.arange(3125, dtype=jnp.int32)
        src = jnp.concatenate([_s, _d, _loop])
        dst = jnp.concatenate([_d, _s, _loop])
        _o = jnp.argsort(dst, stable=True)
        src = src[_o]
        dst = dst[_o]
        edge_attr_16 = jax.random.uniform(jax.random.fold_in(_gk, 11), (103125, 16), jnp.float32, 0.0, 1)
        return (x, src, dst, edge_attr_16)
    x, src, dst, edge_attr_16 = _rec_inputs()

    def _L0_gnn_setup():
        import jax, jax.numpy as jnp
        import numpy as np
        N_NODES = 3125
        N_EDGES = 50000
        EMB = 128
        EDGE_F = 16
        BN_EPS = 1e-05

        def _gin_conv(x, src, dst, edge_attr, w1, b1, bn_w, bn_b, w2, b2, ew, eb):
            edge_emb = edge_attr @ ew.T + eb
            n = x.shape[0]
            agg_x = jax.ops.segment_sum(x[src], dst, num_segments=n) + x
            agg_e = jax.ops.segment_sum(edge_emb, dst, num_segments=n) + eb
            h = jnp.concatenate([agg_x, agg_e], axis=1)
            h = h @ w1.T + b1
            mean = jnp.mean(h, axis=0)
            var = jnp.mean((h - mean) ** 2, axis=0)
            h = (h - mean) * jax.lax.rsqrt(var + BN_EPS) * bn_w + bn_b
            h = jax.nn.relu(h)
            return h @ w2.T + b2
        key = jax.random.key(seed)
        ks = jax.random.split(key, 12)
        s = 0.05
        x = jax.random.normal(ks[0], (N_NODES, EMB), jnp.float32)
        edge_attr = jax.random.uniform(ks[1], (N_EDGES, EDGE_F), jnp.float32)
        edge_index = jax.random.randint(ks[2], (2, N_EDGES), 0, N_NODES, jnp.int32)
        W1 = jax.random.normal(ks[3], (5, 2 * EMB, 2 * EMB), jnp.float32) * s
        B1 = jax.random.normal(ks[4], (5, 2 * EMB), jnp.float32) * s
        BNW = jax.random.uniform(ks[5], (5, 2 * EMB), jnp.float32, 0.5, 1.5)
        BNB = jax.random.normal(ks[6], (5, 2 * EMB), jnp.float32) * s
        W2 = jax.random.normal(ks[7], (5, EMB, 2 * EMB), jnp.float32) * s
        B2 = jax.random.normal(ks[8], (5, EMB), jnp.float32) * s
        EW = jax.random.normal(ks[9], (5, EMB, EDGE_F), jnp.float32) * s
        EB = jax.random.normal(ks[10], (5, EMB), jnp.float32) * s
        return {'x': x, 'edge_attr': edge_attr, 'W1': W1, 'B1': B1, 'BNW': BNW, 'BNB': BNB, 'W2': W2, 'B2': B2, 'EW': EW, 'EB': EB, 'edge_index': edge_index}
    _L0_gnn_all = _L0_gnn_setup()
    _L0_gnn_in = {k: v for k, v in _L0_gnn_all.items() if k in ('W1', 'B1', 'BNW', 'BNB', 'W2', 'B2', 'EW', 'EB')}
    del _L0_gnn_all
    return {'x': x, 'src': src, 'dst': dst, 'edge_attr_16': edge_attr_16, 'L0_gnn_W1': _L0_gnn_in['W1'], 'L0_gnn_B1': _L0_gnn_in['B1'], 'L0_gnn_BNW': _L0_gnn_in['BNW'], 'L0_gnn_BNB': _L0_gnn_in['BNB'], 'L0_gnn_W2': _L0_gnn_in['W2'], 'L0_gnn_B2': _L0_gnn_in['B2'], 'L0_gnn_EW': _L0_gnn_in['EW'], 'L0_gnn_EB': _L0_gnn_in['EB']}

def reference(x, src, dst, edge_attr_16, L0_gnn_W1, L0_gnn_B1, L0_gnn_BNW, L0_gnn_BNB, L0_gnn_W2, L0_gnn_B2, L0_gnn_EW, L0_gnn_EB):
    import jax
    import jax.numpy as jnp

    def _L0_gnn_ref(x, edge_attr, W1, B1, BNW, BNB, W2, B2, EW, EB, edge_index):
        import jax, jax.numpy as jnp
        import numpy as np
        N_NODES = 3125
        N_EDGES = 50000
        EMB = 128
        EDGE_F = 16
        BN_EPS = 1e-05

        def _gin_conv(x, src, dst, edge_attr, w1, b1, bn_w, bn_b, w2, b2, ew, eb):
            edge_emb = edge_attr @ ew.T + eb
            n = x.shape[0]
            agg_x = jax.ops.segment_sum(x[src], dst, num_segments=n) + x
            agg_e = jax.ops.segment_sum(edge_emb, dst, num_segments=n) + eb
            h = jnp.concatenate([agg_x, agg_e], axis=1)
            h = h @ w1.T + b1
            mean = jnp.mean(h, axis=0)
            var = jnp.mean((h - mean) ** 2, axis=0)
            h = (h - mean) * jax.lax.rsqrt(var + BN_EPS) * bn_w + bn_b
            h = jax.nn.relu(h)
            return h @ w2.T + b2
        src, dst = (edge_index[0], edge_index[1])
        h = x
        for l in range(5):
            h = _gin_conv(h, src, dst, edge_attr, W1[l], B1[l], BNW[l], BNB[l], W2[l], B2[l], EW[l], EB[l])
            if l < 4:
                h = jax.nn.relu(h)
        return h
    edge_index = jnp.stack([src, dst])
    h = jnp.maximum(_layernorm(x, axis=-1), 0.0)
    x = x + _L0_gnn_ref(h, edge_attr_16, L0_gnn_W1, L0_gnn_B1, L0_gnn_BNW, L0_gnn_BNB, L0_gnn_W2, L0_gnn_B2, L0_gnn_EW, L0_gnn_EB, edge_index)
    return x

_drawn_inputs = setup_inputs


def setup_inputs(seed=0):
    import zlib

    import numpy as np

    out = dict(_drawn_inputs(seed))
    spreads = {}
    factors = {}
    for name, (base, spread) in spreads.items():
        noise = np.random.default_rng([zlib.crc32(name.encode()), seed]).standard_normal(out[name].shape)
        drawn = base * np.exp(spread * noise) if base else spread * noise
        out[name] = jnp.asarray(drawn.astype(out[name].dtype))
    for name, factor in factors.items():
        out[name] = (out[name] * factor).astype(out[name].dtype)
    return out
```

```python
import concourse.bass as bass
from concourse import mybir
from contextlib import ExitStack

P = 128
N_NODES, D = 3125, 128
N_EDGES, EDGE_F = 103125, 16
HID = 2 * D
LAYERS = 5
EPS = 1e-5

NODE_TILES = -(-N_NODES // P)
LAST_ROWS = N_NODES - (NODE_TILES - 1) * P
GROUP = 16
GROUPS = -(-N_NODES // GROUP)
COLS = GROUPS * GROUP
GCOLS = NODE_TILES * GROUP
GKEY = 512
WINDOW = 6
EDGE_TILES = -(-N_EDGES // P)
SELF_TILE = EDGE_TILES + WINDOW
BATCHES = -(-(SELF_TILE + NODE_TILES) // WINDOW)
PAD_TILES = BATCHES * WINDOW
EXACT = 256
REC = 1 + EDGE_F
UNROLL = 4
ROUNDS = GROUPS // UNROLL
CHUNKS = 7
CW = COLS // CHUNKS
LAST_CW = N_NODES - (CHUNKS - 1) * CW
UNITS = -(-NODE_TILES // 4)
UW = 4 * P
TERMS = 6
SK = TERMS * REC
PIECES = 3

ALU = mybir.AluOpType
ACT = mybir.ActivationFunctionType
F32, BF16, FP16, I32 = mybir.dt.float32, mybir.dt.bfloat16, mybir.dt.float16, mybir.dt.int32
AX = mybir.AxisListType

W1A, W2T, B1, BNW, BNB, B2 = 0, 256, 512, 514, 516, 518
WP_COLS = 646
W1B, EWB = 0, 256
MP_COLS = 256 + SK
ds = bass.ds


def gin_program(nc, x, src, dst, attr, consts, wpack, mpack, out, s_dram, window_dram, rest_dram):
    assert GROUPS % UNROLL == 0 and COLS % CHUNKS == 0 and CHUNKS % 2 == 1 and UNITS % 2 == 1
    with ExitStack() as whole:
        def sem(name):
            return whole.enter_context(nc.semaphore(name))

        def sb(ctx, name, shape, dt):
            return ctx.enter_context(nc.sbuf_tensor(name, shape, dt))

        banks = [whole.enter_context(nc.psum_tensor(f"bank{i}", [P, 512], F32)) for i in range(8)]
        adj_t = sb(whole, "adj", [P, NODE_TILES * COLS], BF16)
        adj = adj_t[:, :].rearrange("p (k c) -> p k c", k=NODE_TILES)
        hp_t = sb(whole, "h_pieces", [P, NODE_TILES * PIECES * D], BF16)
        hp = hp_t[:, :].rearrange("p (k s f) -> p k s f", k=NODE_TILES, s=PIECES)

        flag = sb(whole, "flag", [1, 1], I32)

        with ExitStack() as ctx:
            keys = sb(ctx, "keys", [P, PAD_TILES, 3], F32)
            rhs_oh = sb(ctx, "rhs_onehot", [P, 2, WINDOW, GCOLS], BF16)
            lo_oh = sb(ctx, "lo_onehot", [P, 2, WINDOW, P], BF16)
            dst_oh = sb(ctx, "dst_onehot", [P, 2, WINDOW, GROUP], F32)
            attr_ring = sb(ctx, "attr_ring", [P, UNROLL, WINDOW * REC], F32)
            key_ring = sb(ctx, "key_ring", [P, UNROLL, WINDOW * 3], F32)
            rel = sb(ctx, "rel_keys", [P, 2, WINDOW, 2], F32)
            group_key = sb(ctx, "group_key", [P, GROUPS], F32)
            iota_g = sb(ctx, "iota_g", [P, GCOLS], FP16)
            iota_lo = sb(ctx, "iota_lo", [P, P], FP16)
            iota_d = sb(ctx, "iota_d", [P, GROUP], F32)
            ident = sb(ctx, "ident", [P, P], BF16)
            sring = sb(ctx, "s_ring", [REC, UNROLL * GROUP], F32)
            window_row = sb(ctx, "window_row", [1, 2 * P], I32)
            thr = sb(ctx, "thr", [P, 2], F32)
            count = sb(ctx, "count", [P, 2], F32)
            window_i = sb(ctx, "window_i", [P, 2], I32)
            ln_stats = sb(ctx, "ln_stats", [P, NODE_TILES, 6], F32)
            ln_mv = sb(ctx, "ln_mv", [P, NODE_TILES, 2], F32)
            ln_sd = sb(ctx, "ln_sd", [P, NODE_TILES], F32)
            ln_rstd = sb(ctx, "ln_rstd", [P, NODE_TILES], F32)
            eps_t = sb(ctx, "ln_eps", [P, 1], F32)
            ones = sb(ctx, "ones", [P, 1], F32)
            degs = sb(ctx, "degrees", [ROUNDS, UNROLL * GROUP], F32)
            deg_big = sb(ctx, "degrees_big", [ROUNDS, UNROLL * GROUP], F32)
            deg_stat = sb(ctx, "degree_stats", [ROUNDS, 2], F32)
            missing = sb(ctx, "missing", [1, 1], F32)
            rest = sb(ctx, "count_rest", [P, GCOLS], BF16)

            words = adj_t[:, :].bitcast(I32)
            wordsf = adj_t[:, :].bitcast(F32)
            cut = [0]

            def stage(n, f32=False):
                a = cut[0]
                cut[0] += n
                return (wordsf if f32 else words)[:, a:a + n]

            src_i, dst_i = stage(PAD_TILES), stage(PAD_TILES)
            lo_i, hi_i, grp_i, mod_i = (stage(PAD_TILES) for _ in range(4))
            dkey_i = stage(PAD_TILES)
            first_i = stage(EDGE_TILES)
            first_f = stage(EDGE_TILES, True)
            less0, less1 = stage(EDGE_TILES, True), stage(EDGE_TILES, True)
            x_st = stage(NODE_TILES * D, True).rearrange("p (k f) -> p k f", k=NODE_TILES)
            r_st = stage(NODE_TILES * D, True).rearrange("p (k f) -> p k f", k=NODE_TILES)

            s_idx = sem("indices_loaded")
            s_first = sem("firsts_loaded")
            s_x = sem("x_loaded")
            s_zero = sem("x_pad_zeroed")
            s_const = sem("constants_made")
            s_chain = sem("dve_chain")
            s_keys = sem("keys_made")
            s_count = sem("window_counted")
            s_wd = sem("window_stored")
            s_wr = sem("window_row_loaded")
            s_mv = sem("ln_moments")
            s_sd = sem("ln_deviation")
            s_y = sem("ln_normalised")
            s_hi = sem("ln_high_piece")
            s_r = sem("ln_rest")
            hp_done = sem("h_pieces_done")

            def units(view, u):
                return view[:, 4 * u:min(4 * u + 4, NODE_TILES)]

            with nc.Block() as block:
                @block.sync
                def _(sp):
                    sp.dma_start(dst_i, dst).then_inc(s_idx, 16)
                    sp.dma_start(src_i, src).then_inc(s_idx, 16)
                    sp.dma_start(first_i, dst[0:1, 0:EDGE_TILES].partition_broadcast(P)).then_inc(s_first, 16)
                    sp.wait_ge(s_count, 1)
                    sp.dma_start(window_dram.rearrange("(p h) -> p h", h=2), window_i[:, :]).then_inc(s_wd, 16)
                    sp.wait_ge(s_wd, 16)
                    sp.dma_start(window_row[:, :], window_dram.rearrange("(a n) -> a n", a=1)).then_inc(s_wr, 16)
                    sp.wait_ge(s_wr, 16)

                @block.scalar
                def _(act):
                    act.dma_start(x_st[:, 0:NODE_TILES - 1, :],
                                  x[0:(NODE_TILES - 1) * P, :].rearrange("(k p) f -> p k f", p=P)).then_inc(s_x, 16)
                    act.wait_ge(s_zero, 1)
                    act.dma_start(x_st[0:LAST_ROWS, NODE_TILES - 1, :],
                                  x[(NODE_TILES - 1) * P:N_NODES, :]).then_inc(s_x, 16)
                    act.wait_ge(s_mv, 1)
                    act.wait_ge(s_const, 1)
                    nc.scalar.activation(ln_sd[:, :], ln_mv[:, :, 1], ACT.Sqrt, bias=eps_t[:, 0:1]).then_inc(s_sd, 1)
                    for u in range(UNITS):
                        act.wait_ge(s_y, u + 1)
                        nc.scalar.activation(units(hp, u)[:, :, 0, :], units(x_st, u), ACT.Relu).then_inc(s_hi, 1)

                @block.gpsimd
                def _(pool):
                    nc.gpsimd.memset(x_st[:, NODE_TILES - 1, :], 0.0).then_inc(s_zero, 1)
                    nc.gpsimd.memset(eps_t[:, :], EPS)
                    nc.gpsimd.memset(ones[:, :], 1.0)
                    nc.gpsimd.memset(ident[:, :], 0.0).then_inc(s_zero, 1)
                    nc.gpsimd.iota(thr[:, :], [[GROUP, 2]], base=0, channel_multiplier=2 * GROUP,
                                   allow_small_or_imprecise_dtypes=True)
                    nc.gpsimd.iota(group_key[:, :], [[GKEY, GROUPS]], base=0, channel_multiplier=0,
                                   allow_small_or_imprecise_dtypes=True)
                    nc.gpsimd.iota(iota_g[:, :], [[1, GCOLS]], base=0, channel_multiplier=0,
                                   allow_small_or_imprecise_dtypes=True)
                    nc.gpsimd.iota(iota_lo[:, :], [[1, P]], base=0, channel_multiplier=0,
                                   allow_small_or_imprecise_dtypes=True)
                    nc.gpsimd.iota(iota_d[:, :], [[1, GROUP]], base=0, channel_multiplier=0,
                                   allow_small_or_imprecise_dtypes=True).then_inc(s_const, 1)
                    pool.wait_ge(s_zero, 2)
                    nc.gpsimd.affine_select(out=ident[:, :], in_=ident[:, :], compare_op=ALU.not_equal, fill=1.0,
                                            base=0, pattern=[[-1, P]], channel_multiplier=1).then_inc(s_const, 1)
                    for u in range(UNITS):
                        pool.wait_ge(s_r, u + 1)
                        nc.gpsimd.tensor_tensor(units(hp, u)[:, :, 2, :], units(r_st, u), units(hp, u)[:, :, 1, :],
                                                ALU.subtract).then_inc(hp_done, 1)

                @block.vector
                def _(dve):
                    steps = [0]

                    def then(ins):
                        steps[0] += 1
                        ins.then_inc(s_chain, 1)
                        dve.wait_ge(s_chain, steps[0])

                    V = nc.vector
                    dve.wait_ge(s_first, 16)
                    dve.wait_ge(s_const, 1)
                    then(V.tensor_copy(first_f, first_i))
                    V.tensor_scalar(less0, first_f, thr[:, 0:1], None, ALU.is_lt, ALU.add, accum_out=count[:, 0:1])
                    then(V.tensor_scalar(less1, first_f, thr[:, 1:2], None, ALU.is_lt, ALU.add, accum_out=count[:, 1:2]))
                    V.tensor_scalar(window_i[:, :], count[:, :], -1.0, 0.0, ALU.add, ALU.max).then_inc(s_count, 1)
                    dve.wait_ge(s_idx, 32)
                    V.tensor_scalar(lo_i, src_i, 127, None, ALU.bitwise_and)
                    V.tensor_scalar(hi_i, src_i, 7, 4, ALU.logical_shift_right, ALU.logical_shift_left)
                    V.tensor_scalar(grp_i, dst_i, 4, 9, ALU.arith_shift_right, ALU.logical_shift_left)
                    then(V.tensor_scalar(mod_i, dst_i, 15, None, ALU.bitwise_and))
                    V.tensor_tensor(dkey_i, grp_i, mod_i, ALU.bitwise_or)
                    then(V.tensor_copy(keys[:, :, 2], lo_i))
                    then(V.tensor_copy(keys[:, :, 1], dkey_i))
                    V.tensor_tensor(keys[:, :, 0], keys[:, :, 1], hi_i, ALU.add).then_inc(s_keys, 1)
                    dve.wait_ge(s_x, 32)
                    dve.wait_ge(s_zero, 1)
                    for k in range(NODE_TILES):
                        last = V.bn_stats(ln_stats[:, k, :], x_st[:, k, :])
                    then(last)
                    for k in range(NODE_TILES):
                        last = V.bn_aggr(ln_mv[:, k, :], ln_stats[:, k, :])
                    last.then_inc(s_mv, 1)
                    dve.wait_ge(s_sd, 1)
                    then(V.reciprocal(ln_rstd[:, :], ln_sd[:, :]))
                    for u in range(UNITS):
                        for k in range(4 * u, min(4 * u + 4, NODE_TILES)):
                            last = V.tensor_scalar(x_st[:, k, :], x_st[:, k, :], ln_mv[:, k, 0:1], ln_rstd[:, k:k + 1],
                                                   ALU.subtract, ALU.mult)
                        last.then_inc(s_y, 1)
                    for u in range(UNITS):
                        dve.wait_ge(s_y, u + 1)
                        dve.wait_ge(s_hi, u + 1)
                        then(V.scalar_tensor_tensor(units(r_st, u), units(x_st, u), 0.0, units(hp, u)[:, :, 0, :],
                                                    ALU.max, ALU.subtract))
                        V.tensor_copy(units(hp, u)[:, :, 1, :], units(r_st, u)).then_inc(s_r, 1)

            s_win = [sem(f"window_loaded{u}") for u in range(UNROLL)]
            s_rel = sem("rel_keys_made")
            s_oh = sem("onehots_made")
            s_cnt = sem("group_counted")
            s_ev = sem("group_evacuated")
            s_st = [sem(f"s_stored{h}") for h in range(2)]
            cnt_ps, att_ps = banks[0:2], banks[2:4]

            with nc.Block() as block:
                @block.sync
                def _(sp):
                    def load_round(it, first):
                        starts = [sp.value_load(window_row[0:1, ds(it * UNROLL + u, 1)], min_val=0,
                                                max_val=EDGE_TILES - 1) for u in range(UNROLL)]
                        for u in range(UNROLL):
                            if not first:
                                sp.wait_ge(s_cnt, (it - 1) * UNROLL + u + 1)
                            sp.dma_start(key_ring[:, u, :],
                                         keys[:, :, :].rearrange("p j c -> p (j c)")[:, ds(starts[u] * 3, WINDOW * 3)]
                                         ).then_inc(s_win[u], 16)
                            sp.dma_start(attr_ring[:, u, :], attr[:, ds(starts[u] * REC, WINDOW * REC)]
                                         ).then_inc(s_win[u], 16)
                    load_round(0, True)
                    with sp.Fori(1, ROUNDS) as it:
                        load_round(it, False)

                @block.gpsimd
                def _(pool):
                    def round_(it, first):
                        for u in range(UNROLL):
                            g = it * UNROLL + u
                            pool.wait_ge(s_win[u], (it + 1) * 32)
                            if not (first and u < 2):
                                pool.wait_ge(s_oh, g - 1)
                            nc.gpsimd.tensor_tensor(
                                rel[:, u % 2], key_ring[:, u, :].rearrange("p (j c) -> p j c", c=3)[:, :, 0:2],
                                group_key[:, ds(g, 1)].unsqueeze(1).to_broadcast([P, WINDOW, 2]),
                                ALU.subtract).then_inc(s_rel, 1)
                    round_(0, True)
                    with pool.Fori(1, ROUNDS) as it:
                        round_(it, False)

                @block.vector
                def _(dve):
                    def round_(it, first):
                        for u in range(UNROLL):
                            g = it * UNROLL + u
                            b = u % 2
                            dve.wait_ge(s_rel, g + 1)
                            if not (first and u < 2):
                                dve.wait_ge(s_cnt, g - 1)
                            for j in range(WINDOW):
                                nc.vector.tensor_scalar(rhs_oh[:, b, j, :], iota_g[:, :], rel[:, b, j, 0:1], None,
                                                        ALU.is_equal)
                                nc.vector.tensor_scalar(lo_oh[:, b, j, :], iota_lo[:, :],
                                                        key_ring[:, u, 3 * j + 2:3 * j + 3], None, ALU.is_equal)
                            nc.vector.tensor_tensor(dst_oh[:, b],
                                                    iota_d[:, :].unsqueeze(1).to_broadcast([P, WINDOW, GROUP]),
                                                    rel[:, b, :, 1:2].to_broadcast([P, WINDOW, GROUP]),
                                                    ALU.is_equal).then_inc(s_oh, 1)
                    round_(0, True)
                    with dve.Fori(1, ROUNDS) as it:
                        round_(it, False)

                @block.tensor
                def _(pe):
                    def round_(it, first):
                        for u in range(UNROLL):
                            g = it * UNROLL + u
                            b = u % 2
                            pe.wait_ge(s_oh, g + 1)
                            pe.wait_ge(s_win[u], (it + 1) * 32)
                            if not (first and u < 2):
                                pe.wait_ge(s_ev, g - 1)
                            for j in range(WINDOW):
                                nc.tensor.matmul(cnt_ps[b][:, 0:GCOLS], lo_oh[:, b, j, :], rhs_oh[:, b, j, :],
                                                 start=(j == 0), stop=(j == WINDOW - 1))
                            for j in range(WINDOW):
                                last = nc.tensor.matmul(att_ps[b][0:REC, 0:GROUP],
                                                        attr_ring[:, u, j * REC:(j + 1) * REC], dst_oh[:, b, j, :],
                                                        start=(j == 0), stop=(j == WINDOW - 1))
                            last.then_inc(s_cnt, 1)
                    round_(0, True)
                    with pe.Fori(1, ROUNDS) as it:
                        round_(it, False)

                @block.scalar
                def _(act):
                    def round_(it, first):
                        for u in range(UNROLL):
                            g = it * UNROLL + u
                            b = u % 2
                            act.wait_ge(s_cnt, g + 1)
                            nc.scalar.activation(adj[:, :, ds(g * GROUP, GROUP)],
                                                 cnt_ps[b][:, 0:GCOLS].rearrange("p (k c) -> p k c", c=GROUP), ACT.Copy)
                            if u % 2 == 0 and not first:
                                act.wait_ge(s_st[u // 2], it * 16)
                            nc.scalar.activation(sring[:, u * GROUP:(u + 1) * GROUP], att_ps[b][0:REC, 0:GROUP],
                                                 ACT.Copy).then_inc(s_ev, 1)
                            if u % 2 == 1:
                                act.wait_ge(s_ev, g + 1)
                                act.dma_start(s_dram[:, ds((g - 1) * GROUP, 2 * GROUP)],
                                              sring[:, (u - 1) * GROUP:(u + 1) * GROUP]).then_inc(s_st[u // 2], 16)
                    round_(0, True)
                    with act.Fori(1, ROUNDS) as it:
                        round_(it, False)
                    for h in range(2):
                        act.wait_ge(s_st[h], 16 * ROUNDS)

            s_diag = sem("diagonal_added")
            s_deg = sem("degrees_loaded")
            s_dstat = sem("degree_parts")
            s_dsum = sem("degrees_summed")
            s_flag = sem("flag_made")
            with nc.Block() as block:
                @block.vector
                def _(dve):
                    for k in range(NODE_TILES):
                        w = min(P, COLS - k * P)
                        last = nc.vector.tensor_tensor(adj[:, k, k * P:k * P + w], adj[:, k, k * P:k * P + w],
                                                       ident[:, 0:w], ALU.add)
                    last.then_inc(s_diag, 1)
                    dve.wait_ge(s_deg, 16)
                    nc.vector.tensor_reduce(deg_stat[:, 0:1], degs[:, :], AX.X, ALU.add)
                    nc.vector.tensor_scalar(deg_big[:, :], degs[:, :], float(EXACT), None, ALU.is_ge, ALU.add,
                                            accum_out=deg_stat[:, 1:2]).then_inc(s_dstat, 1)
                    dve.wait_ge(s_dsum, 1)
                    nc.vector.tensor_scalar(missing[:, :], banks[0][0:1, 0:1], float(N_EDGES), None, ALU.not_equal
                                            ).then_inc(s_flag, 1)
                    dve.wait_ge(s_flag, 1)
                    nc.vector.tensor_tensor(missing[:, :], missing[:, :], banks[0][0:1, 1:2], ALU.add).then_inc(s_flag, 1)
                    dve.wait_ge(s_flag, 2)
                    nc.vector.tensor_scalar(flag[:, :], missing[:, :], 0.5, None, ALU.is_ge).then_inc(s_flag, 1)
                    dve.wait_ge(s_diag, 1)
                    dve.wait_ge(s_flag, 3)

                @block.sync
                def _(sp):
                    sp.dma_start(degs[:, :], s_dram[0:1, :].rearrange("a (r c) -> (a r) c", c=UNROLL * GROUP)
                                 ).then_inc(s_deg, 16)

                @block.tensor
                def _(pe):
                    pe.wait_ge(s_dstat, 1)
                    nc.tensor.matmul(banks[0][0:1, 0:2], ones[0:ROUNDS, 0:1], deg_stat[:, :], start=True, stop=True
                                     ).then_inc(s_dsum, 1)

            general = nc.values_load(flag[0:1, 0:1], min_val=0, max_val=1)
            s_gw = sem("general_attr_loaded")
            s_goh = sem("general_onehots_made")
            s_gcnt = sem("general_batch_counted")
            s_gev = sem("general_group_evacuated")
            s_grel = sem("general_rel_keys_made")
            s_grest = sem("general_rest_made")
            s_gst = sem("general_rest_stored")
            s_gsst = sem("general_sums_stored")
            with nc.If(general > 0):
                with nc.Block() as block:
                    @block.sync
                    def _(sp):
                        def load(t):
                            sp.dma_start(attr_ring[:, 0, :], attr[:, ds(t * (WINDOW * REC), WINDOW * REC)]
                                         ).then_inc(s_gw, 16)
                        with sp.Fori(0, GROUPS) as g:
                            load(0)
                            with sp.Fori(1, BATCHES) as t:
                                sp.wait_ge(s_gcnt, g * BATCHES + t)
                                load(t)
                            sp.wait_ge(s_grest, g + 1)
                            sp.dma_start(rest_dram.rearrange("p (k c) -> p k c", k=NODE_TILES)[:, :, ds(g * GROUP, GROUP)],
                                         rest[:, :].rearrange("p (k c) -> p k c", c=GROUP)).then_inc(s_gst, 16)
                            sp.dma_start(s_dram[:, ds(g * GROUP, GROUP)], sring[:, 0:GROUP]).then_inc(s_gsst, 16)
                        sp.wait_ge(s_gst, 16 * GROUPS)
                        sp.wait_ge(s_gsst, 16 * GROUPS)

                    @block.gpsimd
                    def _(pool):
                        with pool.Fori(0, GROUPS) as g:
                            with pool.Fori(0, BATCHES) as t:
                                nc.gpsimd.tensor_tensor(
                                    rel[:, 0], keys[:, ds(t * WINDOW, WINDOW), 0:2],
                                    group_key[:, ds(g, 1)].unsqueeze(1).to_broadcast([P, WINDOW, 2]),
                                    ALU.subtract).then_inc(s_grel, 1)
                                pool.wait_ge(s_goh, g * BATCHES + t + 1)

                    @block.vector
                    def _(dve):
                        with dve.Fori(0, GROUPS) as g:
                            with dve.Fori(0, BATCHES) as t:
                                dve.wait_ge(s_grel, g * BATCHES + t + 1)
                                for j in range(WINDOW):
                                    nc.vector.tensor_scalar(rhs_oh[:, 0, j, :], iota_g[:, :], rel[:, 0, j, 0:1], None,
                                                            ALU.is_equal)
                                    nc.vector.tensor_scalar(lo_oh[:, 0, j, :], iota_lo[:, :],
                                                            keys[:, ds(t * WINDOW + j, 1), 2], None, ALU.is_equal)
                                nc.vector.tensor_tensor(dst_oh[:, 0],
                                                        iota_d[:, :].unsqueeze(1).to_broadcast([P, WINDOW, GROUP]),
                                                        rel[:, 0, :, 1:2].to_broadcast([P, WINDOW, GROUP]),
                                                        ALU.is_equal).then_inc(s_goh, 1)
                                dve.wait_ge(s_gcnt, g * BATCHES + t + 1)
                            dve.wait_ge(s_gev, g + 1)
                            nc.vector.tensor_tensor(rest[:, :].rearrange("p (k c) -> p k c", c=GROUP),
                                                    cnt_ps[0][:, 0:GCOLS].rearrange("p (k c) -> p k c", c=GROUP),
                                                    adj[:, :, ds(g * GROUP, GROUP)], ALU.subtract).then_inc(s_grest, 1)
                            dve.wait_ge(s_gst, (g + 1) * 16)

                    @block.tensor
                    def _(pe):
                        def batch(g, t, first):
                            pe.wait_ge(s_goh, g * BATCHES + t + 1)
                            pe.wait_ge(s_gw, (g * BATCHES + t + 1) * 16)
                            for j in range(WINDOW):
                                nc.tensor.matmul(cnt_ps[0][:, 0:GCOLS], lo_oh[:, 0, j, :], rhs_oh[:, 0, j, :],
                                                 start=(first and j == 0), stop=True, skip_group_check=True)
                            for j in range(WINDOW):
                                last = nc.tensor.matmul(att_ps[0][0:REC, 0:GROUP],
                                                        attr_ring[:, 0, j * REC:(j + 1) * REC], dst_oh[:, 0, j, :],
                                                        start=(first and j == 0), stop=True, skip_group_check=True)
                            last.then_inc(s_gcnt, 1)
                        with pe.Fori(0, GROUPS) as g:
                            batch(g, 0, True)
                            with pe.Fori(1, BATCHES) as t:
                                batch(g, t, False)
                            pe.wait_ge(s_gev, g + 1)
                            pe.wait_ge(s_grest, g + 1)

                    @block.scalar
                    def _(act):
                        def group(g, first):
                            act.wait_ge(s_gcnt, (g + 1) * BATCHES)
                            nc.scalar.activation(adj[:, :, ds(g * GROUP, GROUP)],
                                                 cnt_ps[0][:, 0:GCOLS].rearrange("p (k c) -> p k c", c=GROUP), ACT.Copy)
                            if not first:
                                act.wait_ge(s_gsst, g * 16)
                            nc.scalar.activation(sring[:, 0:GROUP], att_ps[0][0:REC, 0:GROUP], ACT.Copy
                                                 ).then_inc(s_gev, 1)
                        group(0, True)
                        with act.Fori(1, GROUPS) as g:
                            group(g, False)

        with ExitStack() as ctx:
            h1 = sb(ctx, "h1", [P, 2, COLS], F32)
            aggT = sb(ctx, "aggT", [P, CW], F32)
            s6 = sb(ctx, "edge_sums", [SK, COLS], BF16)
            m6 = sb(ctx, "edge_weights", [SK, HID], BF16)
            wp = sb(ctx, "weights", [P, WP_COLS], F32)
            cst = sb(ctx, "const_rows", [P, 8], F32)
            stats = sb(ctx, "bn_stats", [P, 2, CHUNKS * 6], F32)
            small = sb(ctx, "bn_small", [P, 14], F32)
            mv = small[:, 0:4].rearrange("p (h s) -> p h s", h=2)
            sd, rstd, scale, shift, ms = (small[:, a:a + 2] for a in range(4, 14, 2))
            PLUS1, S_A, S_B, M_A, M_B, EPSC = range(6)
            mp = h1[:, 1, COLS - MP_COLS:COLS]
            mt = h1[0:SK, 0, COLS - HID:COLS]
            x_res = hp_t[:, 0:2 * NODE_TILES * D].bitcast(F32).rearrange("p (k f) -> p k f", k=NODE_TILES)

            agg_ps, w2_ps = banks[0:2], banks[2:4]
            w1_ps = [banks[4:6], banks[6:8]]

            l_s = sem("edge_sums_loaded")
            l_c = sem("consts_loaded")
            l_wp = sem("weights_loaded")
            l_mp = sem("edge_weights_loaded")
            l_x = sem("residual_loaded")
            rest_loaded = sem("count_rest_loaded")
            rest_free = sem("count_rest_buffer_free")
            s6_a = sem("edge_sum_pieces_act")
            s6_v = sem("edge_sum_pieces_dve")
            m_ps = sem("edge_weights_product")
            m_c = sem("edge_weight_chain")
            m_done = sem("edge_weight_pieces")
            agg_done = sem("agg_done")
            agg_ev = sem("agg_evacuated")
            w1_done = sem("w1_done")
            h1_ev = sem("h1_evacuated")
            st_done = sem("bn_stats_done")
            mv_done = sem("bn_mv_done")
            sd_done = sem("bn_sd_done")
            bn_c = sem("bn_chain")
            bn_ready = sem("bn_ready")
            relu_done = sem("relu_done")
            w2_done = sem("w2_done")
            t_done = sem("bias_added")
            hi_done = sem("high_piece_done")
            r_done = sem("rest_done")
            mid_done = sem("middle_piece_done")
            o_done = sem("out_added")
            o_st = sem("out_stored")

            S = h1[0:SK, 0, :]
            T = h1[0:SK, 1, :]

            def rest_view(c):
                return h1[:, 0, :].bitcast(BF16)[:, ds(c * (2 * CW), CW)]

            def unit_cols(u):
                return ds(u * UW, UW) if not isinstance(u, int) else slice(u * UW, min((u + 1) * UW, NODE_TILES * P, COLS))

            def tiles_of(u):
                return 1 if isinstance(u, int) and u == UNITS - 1 else 4

            def rows_of(u):
                return LAST_ROWS if isinstance(u, int) and u == UNITS - 1 else P

            def unit_view(half, u):
                k, r = tiles_of(u), rows_of(u)
                if isinstance(u, int) and u == UNITS - 1:
                    return aggT[0:r, half * D:(half + 1) * D].rearrange("p (k f) -> p k f", k=k)
                return h1[0:r, half, ds(u * UW, k * P)].rearrange("p (k f) -> p k f", k=k)

            def w2_view(u, b):
                k, r = tiles_of(u), rows_of(u)
                return w2_ps[b][0:r, 0:k * P].rearrange("p (k f) -> p k f", k=k)

            def hp_view(u, piece):
                k, r = tiles_of(u), rows_of(u)
                return hp[0:r, ds(u * 4, k), piece, :]

            with nc.Block() as block:
                @block.sync
                def _(sp):
                    sp.dma_start(cst[:, :], consts).then_inc(l_c, 16)
                    for t in range(TERMS):
                        sp.dma_start(h1[t * REC:(t + 1) * REC, 0, :], s_dram).then_inc(l_s, 16)

                    def load_layer(l):
                        if not (isinstance(l, int) and l == 0):
                            sp.wait_ge(hp_done, (l + 1) * UNITS)
                        else:
                            sp.wait_ge(s6_a, 3)
                        sp.dma_start(mp, mpack[ds(l, 1)].rearrange("a p c -> (a p) c")).then_inc(l_mp, 16)
                        sp.dma_start(wp[:, :], wpack[ds(l, 1)].rearrange("a p c -> (a p) c")).then_inc(l_wp, 16)
                        with sp.If(general > 0):
                            with sp.Fori(0, CHUNKS) as c:
                                with sp.Fori(0, NODE_TILES) as k:
                                    sp.wait_ge(rest_free, (l * CHUNKS + c) * NODE_TILES + k + 1)
                                    sp.dma_start(rest_view(c), rest_dram[:, ds(k * COLS + c * CW, CW)]
                                                 ).then_inc(rest_loaded, 16)
                    load_layer(0)
                    with sp.Fori(1, LAYERS) as l:
                        load_layer(l)
                    sp.wait_ge(agg_done, LAYERS * CHUNKS)
                    sp.dma_start(x_res[:, 0:NODE_TILES - 1, :],
                                 x[0:(NODE_TILES - 1) * P, :].rearrange("(k p) f -> p k f", p=P)).then_inc(l_x, 16)
                    sp.dma_start(x_res[0:LAST_ROWS, NODE_TILES - 1, :],
                                 x[(NODE_TILES - 1) * P:N_NODES, :]).then_inc(l_x, 16)
                    for u in range(UNITS):
                        sp.wait_ge(o_done, u + 1)
                        if u < UNITS - 1:
                            sp.dma_start(out[u * UW:(u + 1) * UW, :].rearrange("(k p) f -> p k f", p=P),
                                         unit_view(1, u)).then_inc(o_st, 16)
                        else:
                            sp.dma_start(out[u * UW:N_NODES, :], aggT[0:LAST_ROWS, D:2 * D]
                                         ).then_inc(o_st, 16)
                    sp.wait_ge(o_st, 16 * UNITS)

                @block.tensor
                def _(pe):
                    def aggregate(l, c, b):
                        if not (isinstance(c, int) and c < 2):
                            pe.wait_ge(agg_ev, l * CHUNKS + c - 1)
                        def products(k, stop):
                            for s in range(PIECES):
                                last = nc.tensor.matmul(agg_ps[b][:, 0:CW], hp[:, k, s, :], adj[:, k, ds(c * CW, CW)],
                                                        start=(k == 0 and s == 0), stop=stop and s == PIECES - 1)
                            return last
                        for k in range(NODE_TILES - 1):
                            if isinstance(c, int) and c == 0 and k % 4 == 0:
                                pe.wait_ge(hp_done, l * UNITS + k // 4 + 1)
                            products(k, False)
                        if isinstance(c, int) and c == 0:
                            pe.wait_ge(hp_done, (l + 1) * UNITS)
                        with pe.If(general > 0):
                            for k in range(NODE_TILES):
                                pe.wait_ge(rest_loaded, ((l * CHUNKS + c) * NODE_TILES + k + 1) * 16)
                                for s in range(PIECES):
                                    last = nc.tensor.matmul(agg_ps[b][:, 0:CW], hp[:, k, s, :], rest_view(c),
                                                            start=False, stop=False)
                                last.then_inc(rest_free, 1)
                            products(NODE_TILES - 1, True).then_inc(agg_done, 1)
                        with pe.Else():
                            products(NODE_TILES - 1, True).then_inc(agg_done, 1)

                    def hidden(l, c, b):
                        pe.wait_ge(agg_ev, l * CHUNKS + c + 1)
                        if isinstance(c, int) and c == 0:
                            pe.wait_ge(m_done, l + 1)
                            pe.wait_ge(s6_a, 3)
                            pe.wait_ge(l_wp, (l + 1) * 16)
                        if not (isinstance(c, int) and c < 2):
                            pe.wait_ge(h1_ev, l * CHUNKS + c - 1)
                        for h in range(2):
                            nc.tensor.matmul(w1_ps[b][h][:, 0:CW], wp[:, W1A + h * P:W1A + (h + 1) * P], aggT[:, :],
                                             start=True, stop=False)
                            last = nc.tensor.matmul(w1_ps[b][h][:, 0:CW], m6[:, h * P:(h + 1) * P],
                                                    s6[:, ds(c * CW, CW)], start=False, stop=True)
                        last.then_inc(w1_done, 1)

                    def project(l, u, b):
                        pe.wait_ge(relu_done, l * UNITS + u + 1)
                        if u >= 2:
                            pe.wait_ge(t_done, l * UNITS + u - 1)
                        r = rows_of(u)
                        for j in range(tiles_of(u)):
                            for h in range(2):
                                a = u * UW + j * P
                                last = nc.tensor.matmul(w2_ps[b][0:r, j * P:(j + 1) * P], h1[:, h, a:a + r],
                                                        wp[:, W2T + h * P:W2T + (h + 1) * P], start=(h == 0), stop=(h == 1))
                        last.then_inc(w2_done, 1)

                    def layer(l):
                        aggregate(l, 0, 0)
                        pe.wait_ge(l_mp, (l + 1) * 16)
                        nc.tensor.matmul(w2_ps[0][0:SK, 0:HID], mp[:, EWB:EWB + SK], mp[:, W1B:W1B + HID],
                                         start=True, stop=True).then_inc(m_ps, 1)
                        aggregate(l, 1, 1)
                        hidden(l, 0, 0)
                        aggregate(l, 2, 0)
                        hidden(l, 1, 1)
                        with pe.Fori(1, CHUNKS // 2) as i:
                            aggregate(l, 2 * i + 1, 1)
                            hidden(l, 2 * i, 0)
                            aggregate(l, 2 * i + 2, 0)
                            hidden(l, 2 * i + 1, 1)
                        hidden(l, CHUNKS - 1, 0)
                        for u in range(UNITS):
                            project(l, u, u % 2)
                    pe.sem_inc(rest_free, 1)
                    with pe.Fori(0, LAYERS) as l:
                        layer(l)

                @block.scalar
                def _(act):
                    act.wait_ge(s6_v, 1)
                    nc.scalar.activation(s6[:, :], S, ACT.Copy).then_inc(s6_a, 1)
                    act.wait_ge(s6_v, 2)
                    nc.scalar.activation(s6[:, :], T, ACT.Copy).then_inc(s6_a, 1)
                    act.wait_ge(s6_v, 3)
                    nc.scalar.activation(s6[:, :], S, ACT.Copy).then_inc(s6_a, 1)

                    def evac_agg(l, c, b):
                        act.wait_ge(agg_done, l * CHUNKS + c + 1)
                        if not (isinstance(c, int) and c == 0):
                            act.wait_ge(w1_done, l * CHUNKS + c)
                        nc.scalar.activation(aggT[:, :], agg_ps[b][:, 0:CW], ACT.Copy).then_inc(agg_ev, 1)

                    def evac_h1(l, c, b):
                        act.wait_ge(w1_done, l * CHUNKS + c + 1)
                        for h in range(2):
                            last = nc.scalar.activation(h1[:, h, ds(c * CW, CW)], w1_ps[b][h][:, 0:CW], ACT.Identity,
                                                        bias=wp[:, B1 + h:B1 + h + 1])
                        last.then_inc(h1_ev, 1)

                    def relu(l, u):
                        for h in range(2):
                            v = h1[:, h, unit_cols(u)]
                            last = nc.scalar.activation(v, v, ACT.Relu, bias=shift[:, h:h + 1], scale=scale[:, h:h + 1])
                        last.then_inc(relu_done, 1)

                    def layer(l, final):
                        act.wait_ge(l_wp, (l + 1) * 16)
                        evac_agg(l, 0, 0)
                        with act.Fori(0, CHUNKS // 2) as i:
                            evac_agg(l, 2 * i + 1, 1)
                            evac_h1(l, 2 * i, 0)
                            evac_agg(l, 2 * i + 2, 0)
                            evac_h1(l, 2 * i + 1, 1)
                        evac_h1(l, CHUNKS - 1, 0)
                        act.wait_ge(mv_done, l + 1)
                        nc.scalar.activation(sd[:, :], mv[:, :, 1], ACT.Sqrt, bias=cst[:, EPSC:EPSC + 1]).then_inc(sd_done, 1)
                        act.wait_ge(bn_ready, l + 1)
                        for u in range(UNITS + 2):
                            if u < UNITS:
                                relu(l, u)
                            if u >= 2 and not final:
                                act.wait_ge(t_done, l * UNITS + u - 1)
                                nc.scalar.activation(hp_view(u - 2, 0), unit_view(0, u - 2), ACT.Relu).then_inc(hi_done, 1)
                    act.wait_ge(l_c, 16)
                    with act.Fori(0, LAYERS - 1) as l:
                        layer(l, False)
                    layer(LAYERS - 1, True)

                @block.vector
                def _(dve):
                    V = nc.vector
                    dve.wait_ge(l_c, 16)
                    dve.wait_ge(l_s, 16 * TERMS)
                    V.tensor_scalar(S, S, cst[0:SK, PLUS1:PLUS1 + 1], None, ALU.add).then_inc(s6_v, 1)
                    dve.wait_ge(s6_v, 1)
                    dve.wait_ge(s6_a, 1)
                    V.scalar_tensor_tensor(T, s6[:, :], cst[0:SK, S_A:S_A + 1], S, ALU.mult, ALU.add).then_inc(s6_v, 1)
                    dve.wait_ge(s6_v, 2)
                    dve.wait_ge(s6_a, 2)
                    V.scalar_tensor_tensor(S, s6[:, :], cst[0:SK, S_B:S_B + 1], T, ALU.mult, ALU.add).then_inc(s6_v, 1)

                    def edge_weights(l):
                        n = [0]

                        def then(ins):
                            n[0] += 1
                            ins.then_inc(m_c, 1)
                            dve.wait_ge(m_c, l * 5 + n[0])
                        dve.wait_ge(m_ps, l + 1)
                        then(V.tensor_copy(mt[:, :], w2_ps[0][0:SK, 0:HID]))
                        then(V.tensor_copy(m6[:, :], mt[:, :]))
                        then(V.scalar_tensor_tensor(mt[:, :], m6[:, :], cst[0:SK, M_A:M_A + 1], mt[:, :], ALU.mult, ALU.add))
                        then(V.tensor_copy(m6[:, :], mt[:, :]))
                        then(V.scalar_tensor_tensor(mt[:, :], m6[:, :], cst[0:SK, M_B:M_B + 1], mt[:, :], ALU.mult, ALU.add))
                        V.tensor_copy(m6[:, :], mt[:, :]).then_inc(m_done, 1)

                    def bn(l):
                        with dve.Fori(0, CHUNKS - 1) as c:
                            dve.wait_ge(h1_ev, l * CHUNKS + c + 1)
                            for h in range(2):
                                V.bn_stats(stats[:, h, ds(c * 6, 6)], h1[:, h, ds(c * CW, CW)])
                        dve.wait_ge(h1_ev, (l + 1) * CHUNKS)
                        for h in range(2):
                            last = V.bn_stats(stats[:, h, (CHUNKS - 1) * 6:CHUNKS * 6], h1[:, h, (CHUNKS - 1) * CW:N_NODES])
                        last.then_inc(st_done, 1)
                        dve.wait_ge(l_c, 16)
                        dve.wait_ge(st_done, l + 1)
                        for h in range(2):
                            last = V.bn_aggr(mv[:, h, :], stats[:, h, :])
                        last.then_inc(mv_done, 1)
                        dve.wait_ge(sd_done, l + 1)
                        V.reciprocal(rstd[:, :], sd[:, :]).then_inc(bn_c, 1)
                        dve.wait_ge(bn_c, l * 3 + 1)
                        V.tensor_tensor(scale[:, :], rstd[:, :], wp[:, BNW:BNW + 2], ALU.mult).then_inc(bn_c, 1)
                        dve.wait_ge(bn_c, l * 3 + 2)
                        V.tensor_tensor(ms[:, :], mv[:, :, 0], scale[:, :], ALU.mult).then_inc(bn_c, 1)
                        dve.wait_ge(bn_c, l * 3 + 3)
                        V.tensor_tensor(shift[:, :], wp[:, BNB:BNB + 2], ms[:, :], ALU.subtract).then_inc(bn_ready, 1)

                    def b2_like(u):
                        k, r = tiles_of(u), rows_of(u)
                        return wp[0:r, B2:B2 + D].unsqueeze(1).to_broadcast([r, k, D])

                    def add_bias(l, u, b):
                        dve.wait_ge(w2_done, l * UNITS + u + 1)
                        V.tensor_tensor(unit_view(0, u), w2_view(u, b), b2_like(u), ALU.add).then_inc(t_done, 1)

                    def rest(l, u):
                        dve.wait_ge(hi_done, l * UNITS + u + 1)
                        V.scalar_tensor_tensor(unit_view(1, u), unit_view(0, u), 0.0, hp_view(u, 0), ALU.max,
                                               ALU.subtract).then_inc(r_done, 1)
                        dve.wait_ge(r_done, l * UNITS + u + 1)
                        V.tensor_copy(hp_view(u, 1), unit_view(1, u)).then_inc(mid_done, 1)

                    def layer(l, final):
                        edge_weights(l)
                        bn(l)
                        if final:
                            dve.wait_ge(l_x, 32)
                        for u in range(UNITS + 1):
                            if u < UNITS:
                                add_bias(l, u, u % 2)
                            if u >= 1:
                                if final:
                                    dve.wait_ge(t_done, l * UNITS + u)
                                    k, r = tiles_of(u - 1), rows_of(u - 1)
                                    V.tensor_tensor(unit_view(1, u - 1), unit_view(0, u - 1), x_res[0:r, 4 * (u - 1):4 * (u - 1) + k, :],
                                                    ALU.add).then_inc(o_done, 1)
                                else:
                                    rest(l, u - 1)
                    with dve.Fori(0, LAYERS - 1) as l:
                        layer(l, False)
                    layer(LAYERS - 1, True)

                @block.gpsimd
                def _(pool):
                    with pool.Fori(0, LAYERS - 1) as l:
                        for u in range(UNITS):
                            pool.wait_ge(mid_done, l * UNITS + u + 1)
                            nc.gpsimd.tensor_tensor(hp_view(u, 2), unit_view(1, u), hp_view(u, 1),
                                                    ALU.subtract).then_inc(hp_done, 1)


def kernel(x, src, dst, edge_attr_16, L0_gnn_W1, L0_gnn_B1, L0_gnn_BNW, L0_gnn_BNB, L0_gnn_W2, L0_gnn_B2,
           L0_gnn_EW, L0_gnn_EB):
    import numpy as np
    import concourse.bacc as bacc
    from concourse.bass_utils import run_bass_kernel_spmd

    def by_tile(a, fill, own=None):
        a = np.asarray(a)
        pad = np.full((PAD_TILES * P,) + a.shape[1:], fill, a.dtype)
        pad[:N_EDGES] = a
        if own is not None:
            pad[SELF_TILE * P:SELF_TILE * P + N_NODES] = own
        return np.ascontiguousarray(np.moveaxis(pad.reshape((PAD_TILES, P) + a.shape[1:]), 1, 0))

    rec = np.ones((N_EDGES, REC), np.float32)
    rec[:, 1:] = np.asarray(edge_attr_16)
    attr = by_tile(rec, 0).reshape(P, PAD_TILES * REC)

    w1, w2 = np.asarray(L0_gnn_W1), np.asarray(L0_gnn_W2)
    ew, eb = np.asarray(L0_gnn_EW), np.asarray(L0_gnn_EB)
    wpack = np.zeros((LAYERS, P, WP_COLS), np.float32)
    wpack[:, :, W1A:W1A + HID] = w1[:, :, :D].transpose(0, 2, 1)
    wpack[:, :, W2T:W2T + HID] = w2.transpose(0, 2, 1).reshape(LAYERS, 2, P, D).transpose(0, 2, 1, 3).reshape(LAYERS, P, HID)
    for at, v in ((B1, L0_gnn_B1), (BNW, L0_gnn_BNW), (BNB, L0_gnn_BNB)):
        wpack[:, :, at:at + 2] = np.asarray(v).reshape(LAYERS, 2, P).transpose(0, 2, 1)
    wpack[:, :, B2:B2 + D] = np.asarray(L0_gnn_B2)[:, None, :]
    mpack = np.zeros((LAYERS, P, MP_COLS), np.float32)
    mpack[:, :, W1B:W1B + HID] = w1[:, :, D:].transpose(0, 2, 1)
    for t in range(TERMS):
        mpack[:, :, EWB + t * REC] = eb
        mpack[:, :, EWB + t * REC + 1:EWB + (t + 1) * REC] = ew
    consts = np.zeros((P, 8), np.float32)
    for t, (s_piece, m_piece) in enumerate(((0, 0), (0, 1), (0, 2), (1, 0), (1, 1), (2, 0))):
        rows = slice(t * REC, (t + 1) * REC)
        consts[t * REC, 0] = 1.0
        consts[rows, 1] = -1.0 if s_piece >= 1 else 0.0
        consts[rows, 2] = -1.0 if s_piece >= 2 else 0.0
        consts[rows, 3] = -1.0 if m_piece >= 1 else 0.0
        consts[rows, 4] = -1.0 if m_piece >= 2 else 0.0
    consts[:, 5] = EPS

    arrays = {
        "x": np.ascontiguousarray(x), "src": by_tile(src, 0, np.arange(N_NODES)), "dst": by_tile(dst, -1, np.arange(N_NODES)), "attr": attr,
        "consts": consts, "wpack": wpack, "mpack": mpack,
    }
    nc = bacc.Bacc("TRN2", target_bir_lowering=False, num_devices=1)
    ins = [nc.dram_tensor(n, a.shape, mybir.dt.from_np(a.dtype), kind="ExternalInput").ap() for n, a in arrays.items()]
    out = nc.dram_tensor("out", (N_NODES, D), F32, kind="ExternalOutput").ap()
    s_dram = nc.dram_tensor("s_dram", (REC, COLS), F32, kind="Internal").ap()
    window_dram = nc.dram_tensor("window_dram", (2 * P,), I32, kind="Internal").ap()
    rest_dram = nc.dram_tensor("rest_dram", (P, NODE_TILES * COLS), BF16, kind="Internal").ap()
    gin_program(nc, *ins, out, s_dram, window_dram, rest_dram)
    r = run_bass_kernel_spmd(nc, [arrays], core_ids=[0])
    return r.results[0]["out"]
```

```python
import concourse.bass as bass
from concourse import mybir
from contextlib import ExitStack

P = 128
N_NODES, D = 3125, 128
N_EDGES, EDGE_F = 103125, 16
HID = 2 * D
LAYERS = 5
EPS = 1e-5

NODE_TILES = -(-N_NODES // P)
LAST_ROWS = N_NODES - (NODE_TILES - 1) * P
HALF = 8
GROUP = 2 * HALF
GROUPS = -(-N_NODES // GROUP)
COLS = GROUPS * GROUP
HCOLS = NODE_TILES * HALF
HKEY = 256
GKEY = 2 * HKEY
WINDOW = 6
A_TILES, B_FIRST = 4, 1
B_TILES = WINDOW - B_FIRST
EDGE_TILES = -(-N_EDGES // P)
SELF_TILE = EDGE_TILES + WINDOW
BATCH = 4
BATCHES = -(-(SELF_TILE + NODE_TILES) // BATCH)
PAD_TILES = BATCHES * BATCH
REC = 1 + EDGE_F
KREC = 4
UNROLL = 4
RING = 7
PACK = PAD_TILES - WINDOW
ROUNDS = GROUPS // UNROLL
RCOLS = UNROLL * GROUP
EXACT = 256
CHUNKS = 7
CW = COLS // CHUNKS
CROUNDS = ROUNDS // CHUNKS
CGROUPS = CROUNDS * UNROLL
UNITS = -(-NODE_TILES // 4)
UW = 4 * P
TERMS = 6
SK = TERMS * REC
PIECES = 2
LN_SCALE = 1024.0
TOP = 2.0 ** 14

ALU = mybir.AluOpType
ACT = mybir.ActivationFunctionType
F32, BF16, FP16, I32 = mybir.dt.float32, mybir.dt.bfloat16, mybir.dt.float16, mybir.dt.int32
AX = mybir.AxisListType

W1A, W2T, B1, BNW, BNB, B2 = 0, 256, 512, 514, 516, 518
WP_COLS = 646
W1B, EWB = 0, 256
MP_COLS = 256 + SK
PLUS1, S_A, S_B, M_A, M_B, EPSC, ZERO, STACK = 0, 1, 2, 3, 4, 5, 6, 8
C_COLS = STACK + SK
ds = bass.ds


class Steps:

    def __init__(self, engine, sem, base=0):
        self.engine, self.sem, self.base, self.n = engine, sem, base, 0

    def then(self, ins):
        self.n += 1
        ins.then_inc(self.sem, 1)
        self.engine.wait_ge(self.sem, self.base + self.n)


def gin_program(nc, x, src, dst, attr, consts, wpack, mpack, out, keys_dram, deg_dram, window_dram, rest_dram):
    assert GROUPS % UNROLL == 0 and COLS % CHUNKS == 0 and ROUNDS % CHUNKS == 0
    assert CGROUPS % RING == 0 and CGROUPS >= NODE_TILES and CROUNDS >= UNITS
    assert CHUNKS % 2 == 1 and UNITS % 2 == 1 and P % RCOLS == 0
    with ExitStack() as whole:
        def sem(name):
            return whole.enter_context(nc.semaphore(name))

        def sb(ctx, name, shape, dt):
            return ctx.enter_context(nc.sbuf_tensor(name, shape, dt))

        banks = [whole.enter_context(nc.psum_tensor(f"bank{i}", [P, 512], F32)) for i in range(8)]
        adj_t = sb(whole, "adj", [P, NODE_TILES * COLS], BF16)
        adj = adj_t[:, :].rearrange("p (k c) -> p k c", k=NODE_TILES)
        hp_t = sb(whole, "h_pieces", [P, NODE_TILES * PIECES * D], FP16)
        hp = hp_t[:, :].rearrange("p (k s f) -> p k s f", k=NODE_TILES, s=PIECES)
        h1 = sb(whole, "h1", [P, 2, COLS], F32)
        agg0 = h1[:, 1, :]
        s6 = sb(whole, "edge_sums", [SK, COLS], BF16)
        cst = sb(whole, "const_rows", [P, C_COLS], F32)
        wp = sb(whole, "weights", [P, WP_COLS], F32)
        mp = h1[:, 0, COLS - MP_COLS:COLS]
        ident = sb(whole, "ident", [P, P], BF16)
        flag = sb(whole, "flag", [1, 1], I32)

        def units(view, u):
            return view[:, 4 * u:min(4 * u + 4, NODE_TILES)]

        def rest_view(c):
            return h1[:, 0, :].bitcast(BF16)[:, ds(c * (2 * CW), CW)]

        l_c = sem("consts_loaded")
        l_wp = sem("weights_loaded")
        l_mp = sem("edge_weights_loaded")
        hp_done = sem("h_pieces_done")

        with ExitStack() as ctx:
            h1_words = h1[:, 0, :].bitcast(BF16)
            cut16 = [0]

            def carve(n, *shape):
                a = cut16[0]
                cut16[0] += 2 * n
                assert cut16[0] <= 2 * (COLS - MP_COLS)
                return h1_words[:, a:a + 2 * n].rearrange("p (b x) -> p b x", b=2)

            a_oh = carve(HCOLS * A_TILES)
            b_oh = carve(HCOLS * B_TILES)
            lo_oh = carve(P * WINDOW)
            dst_oh = sb(ctx, "dst_onehot", [P, 2, GROUP * WINDOW], F32)
            attr_ring = agg0[:, (CHUNKS - 2) * CW:(CHUNKS - 2) * CW + RING * WINDOW * REC].rearrange(
                "p (s x) -> p s x", s=RING)
            key_ring_t = sb(ctx, "key_ring", [P, RING * WINDOW * KREC], F32)
            key_ring = key_ring_t[:, :].rearrange("p (s x) -> p s x", s=RING)
            rel = sb(ctx, "rel_keys", [P, UNROLL, KREC, WINDOW], BF16)
            group_key = sb(ctx, "group_key", [P, GROUPS], F32)
            iota = sb(ctx, "iota", [P, HCOLS, WINDOW], BF16)
            iota_d = sb(ctx, "iota_d", [P, GROUP, WINDOW], BF16)
            sums = sb(ctx, "sums_ring", [REC, RCOLS], F32)
            st0 = sb(ctx, "stacked_sums", [SK, RCOLS], F32)
            st1 = sb(ctx, "stacked_rest", [SK, RCOLS], F32)
            take = sb(ctx, "stacked_take", [SK, RCOLS], F32)
            piece = sb(ctx, "stacked_piece", [SK, RCOLS], BF16)
            window_row = sb(ctx, "window_row", [1, GROUPS // 2], I32)
            thr = sb(ctx, "thr", [P, 2], F32)
            count = sb(ctx, "count", [P, 2], F32)
            window_f = sb(ctx, "window_f", [P, 2], F32)
            window_i = sb(ctx, "window_i", [P, 1], I32)
            ones = sb(ctx, "ones", [P, 1], F32)
            degs, deg_big = (key_ring_t[0:ROUNDS, i * RCOLS:(i + 1) * RCOLS] for i in range(2))
            deg_stat = sb(ctx, "degree_stats", [ROUNDS, 2], F32)
            missing = sb(ctx, "missing", [1, 1], F32)
            ln_rstd = sb(ctx, "ln_scale", [P, NODE_TILES], F32)
            ln_shift = sb(ctx, "ln_shift", [P, NODE_TILES], F32)

            words = adj_t[:, :].bitcast(I32)
            wordsf = adj_t[:, :].bitcast(F32)
            cut = [0]

            row = COLS // 2

            def stage(n, f32=False):
                if cut[0] % row + n > row - D:
                    cut[0] += row - cut[0] % row
                a = cut[0]
                cut[0] += n
                return (wordsf if f32 else words)[:, a:a + n]

            src_i, dst_i = stage(PAD_TILES), stage(PAD_TILES)
            lo_i, hi_i, half_i, mod_i, or_i, key_i = (stage(PAD_TILES) for _ in range(6))
            keys = h1[:, :, :].rearrange("p h c -> p (h c)")[:, 0:PAD_TILES * KREC].rearrange("p (j c) -> p j c", c=KREC)
            first_i = stage(EDGE_TILES)
            first_f = stage(EDGE_TILES, True)
            less0, less1 = stage(EDGE_TILES, True), stage(EDGE_TILES, True)
            x_st = wordsf.rearrange("p (k c) -> p k c", k=NODE_TILES)[:, :, row - D:]
            ln_stats = stage(NODE_TILES * 6, True).rearrange("p (k s) -> p k s", s=6)
            ln_mv = stage(NODE_TILES * 2, True).rearrange("p (k s) -> p k s", s=2)
            ln_sd, ln_inv = (stage(NODE_TILES, True) for _ in range(2))
            assert cut[0] <= row * NODE_TILES and row - D >= CW // 2

            s_dst = sem("dst_loaded")
            s_src = sem("src_loaded")
            s_first = sem("firsts_loaded")
            s_x = sem("x_loaded")
            s_zero = sem("x_pad_zeroed")
            s_thr = sem("thresholds_made")
            s_const = sem("constants_made")
            s_chain = sem("dve_chain")
            s_lo = sem("source_in_tile_made")
            s_kact = sem("keys_by_act")
            s_kdve = sem("keys_by_dve")
            s_kst = sem("keys_stored")
            s_count = sem("window_counted")
            s_wd = sem("window_stored")
            s_wr = sem("window_row_loaded")
            s_mv = sem("ln_moments")
            s_sd = sem("ln_deviation")
            s_y = sem("ln_normalised")
            s_hi = sem("ln_high_piece")

            with nc.Block() as block:
                @block.sync
                def _(sp):
                    sp.dma_start(first_i, dst[0:1, 0:EDGE_TILES].partition_broadcast(P)).then_inc(s_first, 16)
                    sp.dma_start(dst_i, dst).then_inc(s_dst, 16)
                    sp.dma_start(cst[:, :], consts).then_inc(l_c, 16)
                    sp.dma_start(wp[:, :], wpack[0]).then_inc(l_wp, 16)
                    sp.wait_ge(s_count, 1)
                    sp.dma_start(window_dram.rearrange("(p h) -> p h", h=1), window_i[:, :]).then_inc(s_wd, 16)
                    sp.wait_ge(s_wd, 16)
                    sp.dma_start(window_row[:, :], window_dram[0:GROUPS // 2].rearrange("(a n) -> a n", a=1)).then_inc(s_wr, 16)
                    sp.wait_ge(s_kact, 1)
                    sp.wait_ge(s_kdve, 1)
                    sp.dma_start(keys_dram, keys.rearrange("p j c -> p (j c)")).then_inc(s_kst, 16)
                    sp.wait_ge(s_wr, 16)
                    sp.wait_ge(s_kst, 16)

                @block.scalar
                def _(act):
                    act.dma_start(src_i, src).then_inc(s_src, 16)
                    act.dma_start(x_st[:, 0:NODE_TILES - 1, :],
                                  x[0:(NODE_TILES - 1) * P, :].rearrange("(k p) f -> p k f", p=P)).then_inc(s_x, 16)
                    act.wait_ge(s_zero, 1)
                    act.dma_start(x_st[0:LAST_ROWS, NODE_TILES - 1, :],
                                  x[(NODE_TILES - 1) * P:N_NODES, :]).then_inc(s_x, 16)
                    act.wait_ge(s_dst, 16)
                    nc.scalar.activation(keys[:, :, 2], dst_i, ACT.Copy, scale=float(GKEY // GROUP))
                    act.wait_ge(s_lo, 1)
                    nc.scalar.activation(keys[:, :, 3], lo_i, ACT.Copy).then_inc(s_kact, 1)
                    act.wait_ge(s_mv, 1)
                    act.wait_ge(l_c, 16)
                    nc.scalar.activation(ln_sd, ln_mv[:, :, 1], ACT.Sqrt, bias=cst[:, EPSC:EPSC + 1]).then_inc(s_sd, 1)

                @block.gpsimd
                def _(pool):
                    nc.gpsimd.memset(x_st[:, NODE_TILES - 1, :], 0.0).then_inc(s_zero, 1)
                    nc.gpsimd.iota(thr[:, :], [[GROUP, 2]], base=0, channel_multiplier=2 * GROUP,
                                   allow_small_or_imprecise_dtypes=True).then_inc(s_thr, 1)
                    nc.gpsimd.memset(ident[:, :], 0.0).then_inc(s_zero, 1)
                    nc.gpsimd.memset(ones[:, :], 1.0)
                    nc.gpsimd.iota(group_key[:, :], [[GKEY, GROUPS]], base=0, channel_multiplier=0,
                                   allow_small_or_imprecise_dtypes=True)
                    nc.gpsimd.iota(iota[:, :, :], [[1, HCOLS], [0, WINDOW]], base=0, channel_multiplier=0,
                                   allow_small_or_imprecise_dtypes=True)
                    nc.gpsimd.iota(iota_d[:, :, :], [[GKEY // GROUP, GROUP], [0, WINDOW]], base=0, channel_multiplier=0,
                                   allow_small_or_imprecise_dtypes=True)
                    pool.wait_ge(s_zero, 2)
                    nc.gpsimd.affine_select(out=ident[:, :], in_=ident[:, :], compare_op=ALU.not_equal, fill=1.0,
                                            base=0, pattern=[[-1, P]], channel_multiplier=1).then_inc(s_const, 1)
                    pool.wait_ge(s_const, 1)

                @block.vector
                def _(dve):
                    V = nc.vector
                    steps = Steps(dve, s_chain)
                    dve.wait_ge(s_first, 16)
                    steps.then(V.tensor_copy(first_f, first_i))
                    dve.wait_ge(s_thr, 1)
                    V.tensor_scalar(less0, first_f, thr[:, 0:1], None, ALU.is_lt, ALU.add, accum_out=count[:, 0:1])
                    steps.then(V.tensor_scalar(less1, first_f, thr[:, 1:2], None, ALU.is_lt, ALU.add,
                                               accum_out=count[:, 1:2]))
                    steps.then(V.tensor_scalar(window_f[:, :], count[:, :], -1.0, 0.0, ALU.add, ALU.max))
                    V.scalar_tensor_tensor(window_i[:, :], window_f[:, 1:2], float(PACK), window_f[:, 0:1], ALU.mult,
                                           ALU.add).then_inc(s_count, 1)
                    dve.wait_ge(s_src, 16)
                    dve.wait_ge(s_dst, 16)
                    V.tensor_scalar(lo_i, src_i, P - 1, None, ALU.bitwise_and).then_inc(s_lo, 1)
                    V.tensor_scalar(hi_i, src_i, 7, 3, ALU.logical_shift_right, ALU.logical_shift_left)
                    V.tensor_scalar(half_i, dst_i, 3, 8, ALU.arith_shift_right, ALU.logical_shift_left)
                    steps.then(V.tensor_scalar(mod_i, dst_i, HALF - 1, None, ALU.bitwise_and))
                    steps.then(V.tensor_tensor(or_i, half_i, mod_i, ALU.bitwise_or))
                    steps.then(V.tensor_tensor(key_i, or_i, hi_i, ALU.bitwise_or))
                    V.tensor_copy(keys[:, :, 0], key_i)
                    V.tensor_scalar(keys[:, :, 1], key_i, -float(HKEY), None, ALU.add).then_inc(s_kdve, 1)
                    dve.wait_ge(s_x, 32)
                    dve.wait_ge(s_zero, 1)
                    for k in range(NODE_TILES):
                        last = V.bn_stats(ln_stats[:, k, :], x_st[:, k, :])
                    steps.then(last)
                    for k in range(NODE_TILES):
                        last = V.bn_aggr(ln_mv[:, k, :], ln_stats[:, k, :])
                    last.then_inc(s_mv, 1)
                    dve.wait_ge(s_sd, 1)
                    steps.then(V.reciprocal(ln_inv, ln_sd))
                    steps.then(V.tensor_scalar(ln_rstd[:, :], ln_inv, LN_SCALE, None, ALU.mult))
                    steps.then(V.scalar_tensor_tensor(ln_shift[:, :], ln_mv[:, :, 0], -1.0, ln_rstd[:, :], ALU.mult,
                                                      ALU.mult))

            s_key = [sem(f"key_window_loaded{i}") for i in range(RING)]
            s_attr = [sem(f"attr_window_loaded{i}") for i in range(RING)]
            s_rel = sem("rel_keys_made")
            s_oh = sem("onehots_made")
            s_cnt = sem("group_counted")
            s_ev = sem("group_evacuated")
            s_stack = sem("sums_stacked")
            s_st0 = sem("stacked_sums_out")
            s_deg = sem("degrees_stored")
            s_own = sem("own_edges_added")
            s_pc = sem("pool_chain")
            s_s6 = sem("edge_sum_pieces")
            s_agg0 = sem("first_layer_chunk")
            s_agg0_ev = sem("first_layer_chunk_out")
            cnt_ps, att_ps, stack_ps, agg0_ps = banks[0:2], banks[2:4], banks[4], banks[5]
            CHAIN = 5

            def h_view(t, j):
                return t.rearrange("p (c j) -> p c j", j=j)

            def count_products(b, slot, tiles, first):
                na, nb, b0, wl = (A_TILES, B_TILES, B_FIRST, WINDOW) if tiles is None else (tiles, tiles, 0, tiles)
                av = h_view(a_oh[:, b, 0:HCOLS * na], na)
                bv = h_view(b_oh[:, b, 0:HCOLS * nb], nb)
                lv = h_view(lo_oh[:, b, 0:P * wl], wl)
                dv = h_view(dst_oh[:, b, 0:GROUP * wl], wl)
                for j in range(na):
                    nc.tensor.matmul(cnt_ps[b][:, 0:HCOLS], lv[:, :, j], av[:, :, j], start=(first and j == 0),
                                     stop=(j == na - 1), skip_group_check=True)
                for j in range(nb):
                    nc.tensor.matmul(cnt_ps[b][:, HCOLS:2 * HCOLS], lv[:, :, b0 + j], bv[:, :, j], start=False,
                                     stop=(j == nb - 1), skip_group_check=True)
                for j in range(wl):
                    last = nc.tensor.matmul(att_ps[b][0:REC, 0:GROUP], attr_ring[:, slot, j * REC:(j + 1) * REC],
                                            dv[:, :, j], start=(first and j == 0), stop=(j == wl - 1),
                                            skip_group_check=True)
                return last

            def one_hots(b, u, tiles):
                na, nb, b0, wl = (A_TILES, B_TILES, B_FIRST, WINDOW) if tiles is None else (tiles, tiles, 0, tiles)

                def equal(out, values, key, n, j):
                    return nc.vector.tensor_tensor(h_view(out, j), values[:, 0:n, 0:j],
                                                   key.unsqueeze(1).to_broadcast([P, n, j]), ALU.is_equal)
                equal(a_oh[:, b, 0:HCOLS * na], iota, rel[:, u, 0, 0:na], HCOLS, na)
                equal(b_oh[:, b, 0:HCOLS * nb], iota, rel[:, u, 1, b0:b0 + nb], HCOLS, nb)
                return equal(lo_oh[:, b, 0:P * wl], iota, rel[:, u, 3, 0:wl], P, wl)

            def dst_one_hot(engine, b, u, wl):
                return engine.tensor_tensor(h_view(dst_oh[:, b, 0:GROUP * wl], wl), iota_d[:, :, 0:wl],
                                            rel[:, u, 2, 0:wl].unsqueeze(1).to_broadcast([P, GROUP, wl]), ALU.is_equal)

            def relative(slot, u, g, wl):
                rec = key_ring[:, slot, 0:wl * KREC].rearrange("p (j c) -> p c j", c=KREC)
                nc.gpsimd.tensor_tensor(rel[:, u, 0:3, 0:wl], rec[:, 0:3, :],
                                        group_key[:, ds(g, 1)].unsqueeze(1).to_broadcast([P, 3, wl]), ALU.subtract)
                return nc.gpsimd.tensor_copy(rel[:, u, 3, 0:wl], rec[:, 3, :])

            def out_view(g):
                return adj[:, :, ds(g * GROUP, GROUP)].rearrange("p k (s m) -> p s k m", s=2)

            def bank_view(b):
                return cnt_ps[b][:, 0:2 * HCOLS].rearrange("p (s k m) -> p s k m", s=2, m=HALF)

            def sum_pieces(steps, col, w):
                G = nc.gpsimd

                def column(c):
                    return cst[0:SK, c:c + 1].to_broadcast([SK, w])
                steps.then(G.tensor_tensor(piece[:, 0:w], st0[:, 0:w], column(ZERO), ALU.add))
                steps.then(G.tensor_tensor(take[:, 0:w], piece[:, 0:w], column(S_A), ALU.mult))
                steps.then(G.tensor_tensor(st1[:, 0:w], st0[:, 0:w], take[:, 0:w], ALU.add))
                steps.then(G.tensor_tensor(piece[:, 0:w], st1[:, 0:w], column(ZERO), ALU.add))
                steps.then(G.tensor_tensor(take[:, 0:w], piece[:, 0:w], column(S_B), ALU.mult))
                return G.tensor_tensor(s6[:, ds(col, w)], st1[:, 0:w], take[:, 0:w], ALU.add)

            def agg0_products(k, c, stop):
                for s in range(PIECES):
                    last = nc.tensor.matmul(agg0_ps[:, 0:CW], hp[:, k, s, :], adj[:, k, ds(c * CW, CW)],
                                            start=(k == 0 and s == 0), stop=stop and s == PIECES - 1)
                return last

            def stack_round(pe, r):
                pe.wait_ge(s_ev, (r + 1) * UNROLL)
                nc.tensor.matmul(stack_ps[0:SK, 0:RCOLS], cst[0:REC, STACK:STACK + SK], sums[:, :],
                                 start=True, stop=True).then_inc(s_stack, 1)

            def evac_stack(act, r, first):
                act.wait_ge(s_stack, r + 1)
                if not first:
                    act.wait_ge(s_s6, r)
                    act.wait_ge(s_deg, r * 16)
                nc.scalar.activation(st0[:, :], stack_ps[0:SK, 0:RCOLS], ACT.Identity,
                                     bias=cst[0:SK, PLUS1:PLUS1 + 1]).then_inc(s_st0, 1)
                act.wait_ge(s_st0, r + 1)
                act.dma_start(deg_dram[ds(r, 1), :], st0[0:1, :]).then_inc(s_deg, 16)

            def finish_round(pool, r):
                pool.wait_ge(s_ev, (r + 1) * UNROLL)
                half = r % (P // RCOLS)
                col = r // (P // RCOLS) * COLS + r * RCOLS
                own = adj_t[:, ds(col, RCOLS)]
                nc.gpsimd.tensor_tensor(own, own, ident[:, ds(half * RCOLS, RCOLS)], ALU.add).then_inc(s_own, 1)
                pool.wait_ge(s_st0, r + 1)
                steps = Steps(pool, s_pc, r * CHAIN)
                sum_pieces(steps, r * RCOLS, RCOLS).then_inc(s_s6, 1)
                assert steps.n == CHAIN

            with nc.Block() as block:
                @block.sync
                def _(sp):
                    def load_rings(t, first):
                        starts = []
                        for q in range(RING):
                            pair = sp.value_load(window_row[0:1, ds(t * RING + q, 1)], min_val=0,
                                                 max_val=(EDGE_TILES - 1) * (PACK + 1))
                            starts += [pair % PACK, pair // PACK]
                        for i, start in enumerate(starts):
                            if not (first and i < RING):
                                sp.wait_ge(s_cnt, t * (2 * RING) - RING + i + 1)
                            slot = i % RING
                            sp.dma_start(key_ring[:, slot, :].rearrange("p (j c) -> p j c", c=KREC),
                                         keys_dram.rearrange("p (j c) -> p j c", c=KREC)[:, ds(start, WINDOW), :]
                                         ).then_inc(s_key[slot], 16)
                            sp.dma_start(attr_ring[:, slot, :].rearrange("p (j c) -> p j c", c=REC),
                                         attr.rearrange("p (j c) -> p j c", c=REC)[:, ds(start, WINDOW), :]
                                         ).then_inc(s_attr[slot], 16)
                    load_rings(0, True)
                    with sp.Fori(1, GROUPS // (2 * RING)) as t:
                        load_rings(t, False)

                @block.gpsimd
                def _(pool):
                    def keys(c, i):
                        pool.wait_ge(s_key[i % RING], (c * (CGROUPS // RING) + i // RING + 1) * 16)
                        relative(i % RING, i % UNROLL, c * CGROUPS + i, WINDOW).then_inc(s_rel, 1)

                    def low_piece(u):
                        pool.wait_ge(s_hi, u + 1)
                        nc.gpsimd.tensor_tensor(units(hp, u)[:, :, 1, :], units(x_st, u), units(hp, u)[:, :, 0, :],
                                                ALU.subtract).then_inc(hp_done, 1)

                    def chunk(c, first, last):
                        for i in range(CGROUPS):
                            g = c * CGROUPS + i
                            if not (first and i < 2):
                                pool.wait_ge(s_oh, g - 1)
                            if not (last and i >= CGROUPS - 2):
                                keys(c, i + 2)
                            if i % UNROLL == 2 and not (first and i < UNROLL):
                                finish_round(pool, c * CROUNDS + i // UNROLL - 1)
                            if first and i % UNROLL == UNROLL - 1 and 1 <= i // UNROLL < UNITS:
                                low_piece(i // UNROLL - 1)
                        if first:
                            low_piece(UNITS - 1)
                    keys(0, 0)
                    keys(0, 1)
                    chunk(0, True, False)
                    with pool.Fori(1, CHUNKS - 1) as c:
                        chunk(c, False, False)
                    chunk(CHUNKS - 1, False, True)

                @block.vector
                def _(dve):
                    def round_(r, first):
                        for u in range(UNROLL):
                            g = r * UNROLL + u
                            dve.wait_ge(s_rel, g + 1)
                            if not (first and u < 2):
                                dve.wait_ge(s_cnt, g - 1)
                            one_hots(u % 2, u, None)
                            dst_one_hot(nc.vector, u % 2, u, WINDOW).then_inc(s_oh, 1)
                    round_(0, True)
                    with dve.Fori(1, ROUNDS) as r:
                        round_(r, False)

                @block.tensor
                def _(pe):
                    def chunk(c, first):
                        for i in range(CGROUPS):
                            u = i % UNROLL
                            r = c * CROUNDS + i // UNROLL
                            g = r * UNROLL + u
                            b, slot = u % 2, i % RING
                            if u == 0 and not (first and i == 0):
                                stack_round(pe, r - 1)
                            pe.wait_ge(s_oh, g + 1)
                            pe.wait_ge(s_attr[slot], (c * (CGROUPS // RING) + i // RING + 1) * 16)
                            if not (first and i < 2):
                                pe.wait_ge(s_ev, g - 1)
                            count_products(b, slot, None, True).then_inc(s_cnt, 1)
                            k = i - (CGROUPS - NODE_TILES)
                            if not first and k >= 0:
                                if k == 0:
                                    pe.wait_ge(s_own, c * CROUNDS)
                                    pe.wait_ge(hp_done, UNITS)
                                last = agg0_products(k, c - 1, k == NODE_TILES - 1)
                                if k == NODE_TILES - 1:
                                    last.then_inc(s_agg0, 1)
                    chunk(0, True)
                    with pe.Fori(1, CHUNKS) as c:
                        chunk(c, False)

                @block.scalar
                def _(act):
                    def normalise(k):
                        nc.scalar.activation(x_st[:, k, :], x_st[:, k, :], ACT.Relu, bias=ln_shift[:, k:k + 1],
                                             scale=ln_rstd[:, k:k + 1]).then_inc(s_y, 1)

                    def round_(r, chunk0):
                        for u in range(UNROLL):
                            g = r * UNROLL + u
                            act.wait_ge(s_cnt, g + 1)
                            nc.scalar.activation(out_view(g), bank_view(u % 2), ACT.Copy)
                            nc.scalar.activation(sums[:, u * GROUP:(u + 1) * GROUP], att_ps[u % 2][0:REC, 0:GROUP],
                                                 ACT.Copy).then_inc(s_ev, 1)
                            if u == 0 and not (chunk0 and r == 0):
                                evac_stack(act, r - 1, chunk0 and r == 1)
                            if chunk0 and g < NODE_TILES:
                                normalise(g)
                        if chunk0 and r < UNITS:
                            act.wait_ge(s_y, min((r + 1) * 4, NODE_TILES))
                            nc.scalar.activation(units(hp, r)[:, :, 0, :], units(x_st, r), ACT.Copy).then_inc(s_hi, 1)
                    for r in range(CROUNDS):
                        round_(r, True)
                    with act.Fori(1, CHUNKS) as c:
                        with act.Fori(0, CROUNDS) as q:
                            round_(c * CROUNDS + q, False)
                        act.wait_ge(s_agg0, c)
                        nc.scalar.activation(agg0[:, ds((c - 1) * CW, CW)], agg0_ps[:, 0:CW], ACT.Copy).then_inc(s_agg0_ev, 1)

            s_degl = sem("degrees_loaded")
            s_dstat = sem("degree_parts")
            s_dsum = sem("degrees_summed")
            s_flag = sem("flag_made")
            with nc.Block() as block:
                @block.sync
                def _(sp):
                    sp.dma_start(mp, mpack[0]).then_inc(l_mp, 16)

                @block.tensor
                def _(pe):
                    stack_round(pe, ROUNDS - 1)
                    pe.wait_ge(s_own, ROUNDS)
                    pe.wait_ge(s_agg0_ev, CHUNKS - 1)
                    for k in range(NODE_TILES):
                        last = agg0_products(k, CHUNKS - 1, k == NODE_TILES - 1)
                    last.then_inc(s_agg0, 1)
                    pe.wait_ge(s_dstat, 1)
                    nc.tensor.matmul(banks[0][0:1, 0:2], ones[0:ROUNDS, 0:1], deg_stat[:, :], start=True, stop=True
                                     ).then_inc(s_dsum, 1)

                @block.gpsimd
                def _(pool):
                    finish_round(pool, ROUNDS - 1)
                    pool.wait_ge(s_s6, ROUNDS)

                @block.scalar
                def _(act):
                    evac_stack(act, ROUNDS - 1, False)
                    act.wait_ge(s_deg, ROUNDS * 16)
                    act.dma_start(degs, deg_dram).then_inc(s_degl, 16)
                    act.wait_ge(s_agg0, CHUNKS)
                    nc.scalar.activation(agg0[:, (CHUNKS - 1) * CW:COLS], agg0_ps[:, 0:CW], ACT.Copy).then_inc(s_agg0_ev, 1)
                    act.wait_ge(s_agg0_ev, CHUNKS)

                @block.vector
                def _(dve):
                    V = nc.vector
                    dve.wait_ge(s_degl, 16)
                    V.tensor_reduce(deg_stat[:, 0:1], degs, AX.X, ALU.add)
                    V.tensor_scalar(deg_big, degs, float(EXACT), None, ALU.is_gt, ALU.add,
                                    accum_out=deg_stat[:, 1:2]).then_inc(s_dstat, 1)
                    dve.wait_ge(s_dsum, 1)
                    V.tensor_scalar(missing[:, :], banks[0][0:1, 0:1], float(N_EDGES + COLS), None, ALU.not_equal
                                    ).then_inc(s_flag, 1)
                    dve.wait_ge(s_flag, 1)
                    V.tensor_tensor(missing[:, :], missing[:, :], banks[0][0:1, 1:2], ALU.add).then_inc(s_flag, 1)
                    dve.wait_ge(s_flag, 2)
                    V.tensor_scalar(flag[:, :], missing[:, :], 0.5, None, ALU.is_ge).then_inc(s_flag, 1)
                    dve.wait_ge(s_flag, 3)

            general = nc.values_load(flag[0:1, 0:1], min_val=0, max_val=1)
            rest = a_oh[:, 1, 0:2 * HCOLS]
            s_gw = sem("general_window_loaded")
            s_grel = sem("general_rel_keys_made")
            s_goh = sem("general_onehots_made")
            s_gcnt = sem("general_batch_counted")
            s_gev = sem("general_group_evacuated")
            s_grest = sem("general_rest_made")
            s_gst = sem("general_rest_stored")
            s_gstack = sem("general_sums_stacked")
            s_gst0 = sem("general_stacked_sums_out")
            s_gpc = sem("general_pool_chain")
            s_gs6 = sem("general_edge_sum_pieces")
            s_gload = sem("general_rest_loaded")
            s_gfree = sem("general_rest_buffer_free")
            s_gagg = sem("general_chunk")
            s_gagg_ev = sem("general_chunk_out")
            with nc.If(general > 0):
                with nc.Block() as block:
                    @block.sync
                    def _(sp):
                        def load(t):
                            sp.dma_start(key_ring[:, 0, 0:BATCH * KREC], keys_dram[:, ds(t * (BATCH * KREC), BATCH * KREC)]
                                         ).then_inc(s_gw, 16)
                            sp.dma_start(attr_ring[:, 0, 0:BATCH * REC], attr[:, ds(t * (BATCH * REC), BATCH * REC)]
                                         ).then_inc(s_gw, 16)
                        with sp.Fori(0, GROUPS) as g:
                            load(0)
                            with sp.Fori(1, BATCHES) as t:
                                sp.wait_ge(s_gcnt, g * BATCHES + t)
                                load(t)
                            sp.wait_ge(s_grest, g + 1)
                            for s in range(2):
                                sp.dma_start(rest_dram.rearrange("p (k c) -> p k c", k=NODE_TILES)
                                             [:, :, ds(g * GROUP + s * HALF, HALF)],
                                             rest[:, s * HCOLS:(s + 1) * HCOLS].rearrange("p (k m) -> p k m", m=HALF)
                                             ).then_inc(s_gst, 16)
                        sp.wait_ge(s_gst, 32 * GROUPS)
                        with sp.Fori(0, CHUNKS) as c:
                            with sp.Fori(0, NODE_TILES) as k:
                                sp.wait_ge(s_gfree, c * NODE_TILES + k + 1)
                                sp.dma_start(rest_view(0), rest_dram[:, ds(k * COLS + c * CW, CW)]).then_inc(s_gload, 16)

                    @block.gpsimd
                    def _(pool):
                        with pool.Fori(0, GROUPS) as g:
                            with pool.Fori(0, BATCHES) as t:
                                pool.wait_ge(s_gw, (g * BATCHES + t + 1) * 32)
                                relative(0, 0, g, BATCH).then_inc(s_grel, 1)
                                pool.wait_ge(s_goh, g * BATCHES + t + 1)
                            pool.wait_ge(s_gst0, g + 1)
                            steps = Steps(pool, s_gpc, g * CHAIN)
                            sum_pieces(steps, g * GROUP, GROUP).then_inc(s_gs6, 1)

                    @block.vector
                    def _(dve):
                        with dve.Fori(0, GROUPS) as g:
                            with dve.Fori(0, BATCHES) as t:
                                dve.wait_ge(s_grel, g * BATCHES + t + 1)
                                one_hots(0, 0, BATCH)
                                dst_one_hot(nc.vector, 0, 0, BATCH).then_inc(s_goh, 1)
                                dve.wait_ge(s_gcnt, g * BATCHES + t + 1)
                            dve.wait_ge(s_gev, g + 1)
                            for s in range(2):
                                last = nc.vector.tensor_tensor(
                                    rest[:, s * HCOLS:(s + 1) * HCOLS].rearrange("p (k m) -> p k m", m=HALF),
                                    bank_view(0)[:, s], out_view(g)[:, s], ALU.subtract)
                            last.then_inc(s_grest, 1)
                            dve.wait_ge(s_gst, (g + 1) * 32)

                    @block.tensor
                    def _(pe):
                        def batch(g, t, first):
                            pe.wait_ge(s_goh, g * BATCHES + t + 1)
                            count_products(0, 0, BATCH, first).then_inc(s_gcnt, 1)
                        with pe.Fori(0, GROUPS) as g:
                            batch(g, 0, True)
                            with pe.Fori(1, BATCHES) as t:
                                batch(g, t, False)
                            pe.wait_ge(s_gev, g + 1)
                            nc.tensor.matmul(stack_ps[0:SK, 0:GROUP], cst[0:REC, STACK:STACK + SK], sums[:, 0:GROUP],
                                             start=True, stop=True).then_inc(s_gstack, 1)
                            pe.wait_ge(s_grest, g + 1)
                            pe.wait_ge(s_gst0, g + 1)
                        pe.sem_inc(s_gfree, 1)
                        with pe.Fori(0, CHUNKS) as c:
                            for k in range(NODE_TILES):
                                agg0_products(k, c, False)
                            for k in range(NODE_TILES):
                                pe.wait_ge(s_gload, (c * NODE_TILES + k + 1) * 16)
                                for s in range(PIECES):
                                    last = nc.tensor.matmul(agg0_ps[:, 0:CW], hp[:, k, s, :], rest_view(0), start=False,
                                                            stop=(k == NODE_TILES - 1 and s == PIECES - 1))
                                last.then_inc(s_gfree, 1)
                            pe.wait_ge(s_gfree, (c + 1) * NODE_TILES + 1)
                            nc.tensor.sem_inc(s_gagg, 1)
                            pe.wait_ge(s_gagg_ev, c + 1)

                    @block.scalar
                    def _(act):
                        with act.Fori(0, GROUPS) as g:
                            act.wait_ge(s_gcnt, (g + 1) * BATCHES)
                            nc.scalar.activation(out_view(g), bank_view(0), ACT.Copy)
                            nc.scalar.activation(sums[:, 0:GROUP], att_ps[0][0:REC, 0:GROUP], ACT.Copy
                                                 ).then_inc(s_gev, 1)
                            act.wait_ge(s_gstack, g + 1)
                            nc.scalar.activation(st0[:, 0:GROUP], stack_ps[0:SK, 0:GROUP], ACT.Identity,
                                                 bias=cst[0:SK, PLUS1:PLUS1 + 1]).then_inc(s_gst0, 1)
                        with act.Fori(0, CHUNKS) as c:
                            act.wait_ge(s_gagg, c + 1)
                            nc.scalar.activation(agg0[:, ds(c * CW, CW)], agg0_ps[:, 0:CW], ACT.Copy).then_inc(s_gagg_ev, 1)

        with ExitStack() as ctx:
            aggT = sb(ctx, "aggT", [P, max(CW, 2 * D)], F32)
            m6 = sb(ctx, "edge_weights", [SK, HID], BF16)
            mt = sb(ctx, "edge_weights_f", [SK, HID], F32)
            uw = sb(ctx, "bound_parts", [P, HID], F32)
            row = sb(ctx, "bound_row", [P, 4, D], F32)
            ones = sb(ctx, "ones2", [P, P], F32)
            inv = sb(ctx, "inverse_scale", [P, 1], F32)
            stats = sb(ctx, "bn_stats", [P, 2, CHUNKS * 6], F32)
            small = sb(ctx, "bn_small", [P, 20], F32)
            mv = small[:, 0:4].rearrange("p (h s) -> p h s", h=2)
            ab = small[:, 4:8]
            sd, rstd, scale, shift, ms, ub = (small[:, a:a + 2] for a in range(8, 20, 2))
            x_res = hp_t[:, 0:2 * NODE_TILES * D].bitcast(F32).rearrange("p (k f) -> p k f", k=NODE_TILES)

            agg_ps, w2_ps = banks[0:2], banks[2:4]
            w1_ps = [banks[4:6], banks[6:8]]

            l_x = sem("residual_loaded")
            rest_loaded = sem("count_rest_loaded")
            rest_free = sem("count_rest_buffer_free")
            ones_done = sem("ones_made")
            m_ps = sem("edge_weights_product")
            m_done = sem("edge_weight_pieces")
            w_chain = sem("weights_chain")
            w1_scaled = sem("w1_scaled")
            uw_done = sem("bound_parts_done")
            bound = sem("bound_summed")
            w2_scaled = sem("w2_scaled")
            agg_done = sem("agg_done")
            agg_ev = sem("agg_evacuated")
            w1_done = sem("w1_done")
            h1_ev = sem("h1_evacuated")
            st_done = sem("bn_stats_done")
            mv_done = sem("bn_mv_done")
            sd_done = sem("bn_sd_done")
            bn_c = sem("bn_chain")
            bn_ready = sem("bn_ready")
            relu_done = sem("relu_done")
            w2_done = sem("w2_done")
            t_done = sem("bias_added")
            hi_done = sem("high_piece_done")
            o_done = sem("out_added")
            o_st = sem("out_stored")
            WSTEPS = 17

            def tiles_of(u):
                return 1 if u == UNITS - 1 else 4

            def rows_of(u):
                return LAST_ROWS if u == UNITS - 1 else P

            def unit_view(half, u):
                k, r = tiles_of(u), rows_of(u)
                if u == UNITS - 1:
                    return aggT[0:r, half * D:(half + 1) * D].rearrange("p (k f) -> p k f", k=k)
                return h1[0:r, half, u * UW:u * UW + k * P].rearrange("p (k f) -> p k f", k=k)

            def w2_view(u):
                k, r = tiles_of(u), rows_of(u)
                return w2_ps[u % 2][0:r, 0:k * P].rearrange("p (k f) -> p k f", k=k)

            def hp_view(u, piece):
                k, r = tiles_of(u), rows_of(u)
                return hp[0:r, u * 4:u * 4 + k, piece, :]

            def later(l):
                return not (isinstance(l, int) and l == 0)

            with nc.Block() as block:
                @block.sync
                def _(sp):
                    def load_layer(l):
                        sp.wait_ge(hp_done, (l + 1) * UNITS)
                        sp.dma_start(mp, mpack[ds(l, 1)].rearrange("a p c -> (a p) c")).then_inc(l_mp, 16)
                        sp.dma_start(wp[:, :], wpack[ds(l, 1)].rearrange("a p c -> (a p) c")).then_inc(l_wp, 16)
                        with sp.If(general > 0):
                            with sp.Fori(0, CHUNKS) as c:
                                with sp.Fori(0, NODE_TILES) as k:
                                    sp.wait_ge(rest_free, ((l - 1) * CHUNKS + c) * NODE_TILES + k + 1)
                                    sp.dma_start(rest_view(c), rest_dram[:, ds(k * COLS + c * CW, CW)]
                                                 ).then_inc(rest_loaded, 16)
                    with sp.Fori(1, LAYERS) as l:
                        load_layer(l)
                    sp.wait_ge(agg_done, (LAYERS - 1) * CHUNKS)
                    sp.dma_start(x_res[:, 0:NODE_TILES - 1, :],
                                 x[0:(NODE_TILES - 1) * P, :].rearrange("(k p) f -> p k f", p=P)).then_inc(l_x, 16)
                    sp.dma_start(x_res[0:LAST_ROWS, NODE_TILES - 1, :],
                                 x[(NODE_TILES - 1) * P:N_NODES, :]).then_inc(l_x, 16)
                    for u in range(UNITS):
                        sp.wait_ge(o_done, u + 1)
                        if u < UNITS - 1:
                            sp.dma_start(out[u * UW:(u + 1) * UW, :].rearrange("(k p) f -> p k f", p=P),
                                         unit_view(1, u)).then_inc(o_st, 16)
                        else:
                            sp.dma_start(out[u * UW:N_NODES, :], aggT[0:LAST_ROWS, D:2 * D]).then_inc(o_st, 16)
                    sp.wait_ge(o_st, 16 * UNITS)

                @block.tensor
                def _(pe):
                    def aggregate(l, c, b):
                        n = (l - 1) * CHUNKS + c
                        if not (isinstance(c, int) and c < 2):
                            pe.wait_ge(agg_ev, n - 1)

                        def products(k, stop):
                            for s in range(PIECES):
                                last = nc.tensor.matmul(agg_ps[b][:, 0:CW], hp[:, k, s, :], adj[:, k, ds(c * CW, CW)],
                                                        start=(k == 0 and s == 0), stop=stop and s == PIECES - 1)
                            return last
                        for k in range(NODE_TILES - 1):
                            if isinstance(c, int) and c == 0 and k % 4 == 0:
                                pe.wait_ge(hp_done, l * UNITS + k // 4 + 1)
                            products(k, False)
                        if isinstance(c, int) and c == 0:
                            pe.wait_ge(hp_done, (l + 1) * UNITS)
                        with pe.If(general > 0):
                            for k in range(NODE_TILES):
                                pe.wait_ge(rest_loaded, (n * NODE_TILES + k + 1) * 16)
                                for s in range(PIECES):
                                    last = nc.tensor.matmul(agg_ps[b][:, 0:CW], hp[:, k, s, :], rest_view(c),
                                                            start=False, stop=False)
                                last.then_inc(rest_free, 1)
                            products(NODE_TILES - 1, True).then_inc(agg_done, 1)
                        with pe.Else():
                            products(NODE_TILES - 1, True).then_inc(agg_done, 1)

                    def hidden(l, c, b):
                        if later(l):
                            pe.wait_ge(agg_ev, (l - 1) * CHUNKS + c + 1)
                        if isinstance(c, int) and c == 0:
                            pe.wait_ge(m_done, l + 1)
                            pe.wait_ge(w1_scaled, l + 1)
                        if not (isinstance(c, int) and c < 2):
                            pe.wait_ge(h1_ev, l * CHUNKS + c - 1)
                        sums_in = aggT[:, 0:CW] if later(l) else agg0[:, c * CW:(c + 1) * CW]
                        for h in range(2):
                            nc.tensor.matmul(w1_ps[b][h][:, 0:CW], wp[:, W1A + h * P:W1A + (h + 1) * P], sums_in,
                                             start=True, stop=False)
                            last = nc.tensor.matmul(w1_ps[b][h][:, 0:CW], m6[:, h * P:(h + 1) * P],
                                                    s6[:, ds(c * CW, CW)], start=False, stop=True)
                        last.then_inc(w1_done, 1)

                    def edge_weights(l):
                        pe.wait_ge(l_mp, (l + 1) * 16)
                        nc.tensor.matmul(w2_ps[0][0:SK, 0:HID], mp[:, EWB:EWB + SK], mp[:, W1B:W1B + HID],
                                         start=True, stop=True).then_inc(m_ps, 1)

                    def bounds(l):
                        pe.wait_ge(uw_done, l + 1)
                        for h in range(2):
                            last = nc.tensor.matmul(w2_ps[1][:, 0:D], ones[:, :], uw[:, h * P:(h + 1) * P],
                                                    start=(h == 0), stop=(h == 1))
                        last.then_inc(bound, 1)

                    def project(l, u, final):
                        if u == 0 and not final:
                            pe.wait_ge(w2_scaled, l + 1)
                        pe.wait_ge(relu_done, l * UNITS + u + 1)
                        if u >= 2:
                            pe.wait_ge(t_done, l * UNITS + u - 1)
                        r = rows_of(u)
                        for j in range(tiles_of(u)):
                            for h in range(2):
                                a = u * UW + j * P
                                last = nc.tensor.matmul(w2_ps[u % 2][0:r, j * P:(j + 1) * P], h1[:, h, a:a + r],
                                                        wp[:, W2T + h * P:W2T + (h + 1) * P], start=(h == 0), stop=(h == 1))
                        last.then_inc(w2_done, 1)

                    def layer(l, final):
                        aggregate(l, 0, 0)
                        edge_weights(l)
                        aggregate(l, 1, 1)
                        hidden(l, 0, 0)
                        aggregate(l, 2, 0)
                        hidden(l, 1, 1)
                        if not final:
                            bounds(l)
                        with pe.Fori(1, CHUNKS // 2) as i:
                            aggregate(l, 2 * i + 1, 1)
                            hidden(l, 2 * i, 0)
                            aggregate(l, 2 * i + 2, 0)
                            hidden(l, 2 * i + 1, 1)
                        hidden(l, CHUNKS - 1, 0)
                        for u in range(UNITS):
                            project(l, u, final)

                    pe.wait_ge(ones_done, 1)
                    pe.sem_inc(rest_free, 1)
                    edge_weights(0)
                    for c in range(CHUNKS):
                        hidden(0, c, c % 2)
                        if c == 1:
                            bounds(0)
                    for u in range(UNITS):
                        project(0, u, False)
                    with pe.Fori(1, LAYERS - 1) as l:
                        layer(l, False)
                    layer(LAYERS - 1, True)

                @block.scalar
                def _(act):
                    def evac_agg(l, c, b):
                        n = (l - 1) * CHUNKS + c
                        act.wait_ge(agg_done, n + 1)
                        if not (isinstance(c, int) and c == 0):
                            act.wait_ge(w1_done, l * CHUNKS + c)
                        nc.scalar.activation(aggT[:, 0:CW], agg_ps[b][:, 0:CW], ACT.Copy).then_inc(agg_ev, 1)

                    def evac_h1(l, c, b):
                        act.wait_ge(w1_done, l * CHUNKS + c + 1)
                        for h in range(2):
                            last = nc.scalar.activation(h1[:, h, ds(c * CW, CW)], w1_ps[b][h][:, 0:CW], ACT.Identity,
                                                        bias=wp[:, B1 + h:B1 + h + 1])
                        last.then_inc(h1_ev, 1)

                    def relu(l, u):
                        for h in range(2):
                            v = h1[:, h, u * UW:min((u + 1) * UW, COLS)]
                            last = nc.scalar.activation(v, v, ACT.Relu, bias=shift[:, h:h + 1], scale=scale[:, h:h + 1])
                        last.then_inc(relu_done, 1)

                    def normalise(l, final):
                        act.wait_ge(mv_done, l + 1)
                        nc.scalar.activation(sd[:, :], mv[:, :, 1], ACT.Sqrt, bias=cst[:, EPSC:EPSC + 1]).then_inc(sd_done, 1)
                        act.wait_ge(bn_ready, l + 1)
                        for u in range(UNITS + 2):
                            if u < UNITS:
                                relu(l, u)
                            if u >= 2 and not final:
                                act.wait_ge(t_done, l * UNITS + u - 1)
                                nc.scalar.activation(hp_view(u - 2, 0), unit_view(0, u - 2), ACT.Relu).then_inc(hi_done, 1)

                    def layer(l, final):
                        act.wait_ge(l_wp, (l + 1) * 16)
                        evac_agg(l, 0, 0)
                        with act.Fori(0, CHUNKS // 2) as i:
                            evac_agg(l, 2 * i + 1, 1)
                            evac_h1(l, 2 * i, 0)
                            evac_agg(l, 2 * i + 2, 0)
                            evac_h1(l, 2 * i + 1, 1)
                        evac_h1(l, CHUNKS - 1, 0)
                        normalise(l, final)

                    for c in range(CHUNKS):
                        evac_h1(0, c, c % 2)
                    normalise(0, False)
                    with act.Fori(1, LAYERS - 1) as l:
                        layer(l, False)
                    layer(LAYERS - 1, True)

                @block.gpsimd
                def _(pool):
                    nc.gpsimd.memset(ones[:, :], 1.0).then_inc(ones_done, 1)

                @block.vector
                def _(dve):
                    V = nc.vector

                    def weights(l, final):
                        steps = Steps(dve, w_chain, l * WSTEPS)
                        dve.wait_ge(l_wp, (l + 1) * 16)
                        w1 = wp[:, W1A:W1A + HID]
                        w2 = wp[:, W2T:W2T + HID].rearrange("p (h f) -> p h f", h=2)
                        if later(l):
                            V.tensor_scalar(w1, w1, inv[:, 0:1], None, ALU.mult).then_inc(w1_scaled, 1)
                        else:
                            V.tensor_scalar(w1, w1, 1.0 / LN_SCALE, None, ALU.mult).then_inc(w1_scaled, 1)
                        dve.wait_ge(m_ps, l + 1)
                        steps.then(V.tensor_copy(mt[:, :], w2_ps[0][0:SK, 0:HID]))
                        steps.then(V.tensor_copy(m6[:, :], mt[:, :]))
                        steps.then(V.scalar_tensor_tensor(mt[:, :], m6[:, :], cst[0:SK, M_A:M_A + 1], mt[:, :], ALU.mult, ALU.add))
                        steps.then(V.tensor_copy(m6[:, :], mt[:, :]))
                        steps.then(V.scalar_tensor_tensor(mt[:, :], m6[:, :], cst[0:SK, M_B:M_B + 1], mt[:, :], ALU.mult, ALU.add))
                        V.tensor_copy(m6[:, :], mt[:, :]).then_inc(m_done, 1)
                        if final:
                            return
                        def absolute(out, v):
                            return V.scalar_tensor_tensor(out, v, -1.0, v, ALU.mult, ALU.max)
                        steps.then(absolute(ab, wp[:, BNW:BNB + 2]))
                        steps.then(V.scalar_tensor_tensor(ub, ab[:, 0:2], float(N_NODES) ** 0.5, ab[:, 2:4], ALU.mult,
                                                          ALU.add))
                        parts = uw[:, :].rearrange("p (h f) -> p h f", h=2)
                        steps.then(absolute(parts, w2))
                        V.tensor_tensor(parts, parts, ub.unsqueeze(2).to_broadcast([P, 2, D]), ALU.mult).then_inc(uw_done, 1)
                        b2 = wp[:, B2:B2 + D]
                        steps.then(absolute(row[:, 0, :], b2))
                        dve.wait_ge(bound, l + 1)
                        steps.then(V.scalar_tensor_tensor(row[:, 1, :], row[:, 0, :], 1e-30, w2_ps[1][:, 0:D], ALU.max,
                                                          ALU.add))
                        steps.then(V.tensor_scalar(row[:, 2, :].bitcast(I32), row[:, 1, :].bitcast(I32), 0x7F800000, None,
                                                   ALU.bitwise_and))
                        steps.then(V.reciprocal(row[:, 3, :], row[:, 2, :]))
                        steps.then(V.tensor_scalar(row[:, 0, :], row[:, 3, :], TOP, None, ALU.mult))
                        steps.then(V.tensor_tensor(b2, b2, row[:, 0, :], ALU.mult))
                        steps.then(V.tensor_tensor(w2, w2, row[:, 0:1, :].to_broadcast([P, 2, D]), ALU.mult))
                        steps.then(V.tensor_scalar(row[:, 3, :], row[:, 2, :], 1.0 / TOP, None, ALU.mult))
                        steps.then(V.tensor_tensor(row[:, 1, :], row[:, 3, :], ident[:, :], ALU.mult))
                        V.tensor_reduce(inv[:, 0:1], row[:, 1, :], AX.X, ALU.add).then_inc(w2_scaled, 1)
                        assert steps.n == WSTEPS

                    def bn(l):
                        with dve.Fori(0, CHUNKS - 1) as c:
                            dve.wait_ge(h1_ev, l * CHUNKS + c + 1)
                            for h in range(2):
                                V.bn_stats(stats[:, h, ds(c * 6, 6)], h1[:, h, ds(c * CW, CW)])
                        dve.wait_ge(h1_ev, (l + 1) * CHUNKS)
                        for h in range(2):
                            last = V.bn_stats(stats[:, h, (CHUNKS - 1) * 6:CHUNKS * 6], h1[:, h, (CHUNKS - 1) * CW:N_NODES])
                        last.then_inc(st_done, 1)
                        dve.wait_ge(l_c, 16)
                        dve.wait_ge(st_done, l + 1)
                        for h in range(2):
                            last = V.bn_aggr(mv[:, h, :], stats[:, h, :])
                        last.then_inc(mv_done, 1)
                        dve.wait_ge(sd_done, l + 1)
                        steps = Steps(dve, bn_c, l * 3)
                        steps.then(V.reciprocal(rstd, sd))
                        steps.then(V.tensor_tensor(scale, rstd, wp[:, BNW:BNW + 2], ALU.mult))
                        steps.then(V.tensor_tensor(ms, mv[:, :, 0], scale, ALU.mult))
                        V.tensor_tensor(shift, wp[:, BNB:BNB + 2], ms, ALU.subtract).then_inc(bn_ready, 1)

                    def add_bias(l, u):
                        k, r = tiles_of(u), rows_of(u)
                        dve.wait_ge(w2_done, l * UNITS + u + 1)
                        V.tensor_tensor(unit_view(0, u), w2_view(u),
                                        wp[0:r, B2:B2 + D].unsqueeze(1).to_broadcast([r, k, D]), ALU.add).then_inc(t_done, 1)

                    def low_piece(l, u):
                        dve.wait_ge(hi_done, l * UNITS + u + 1)
                        V.scalar_tensor_tensor(hp_view(u, 1), unit_view(0, u), 0.0, hp_view(u, 0), ALU.max,
                                               ALU.subtract).then_inc(hp_done, 1)

                    def residual(l, u):
                        k, r = tiles_of(u), rows_of(u)
                        dve.wait_ge(t_done, l * UNITS + u + 1)
                        V.tensor_tensor(unit_view(1, u), unit_view(0, u), x_res[0:r, 4 * u:4 * u + k, :],
                                        ALU.add).then_inc(o_done, 1)

                    def layer(l, final):
                        weights(l, final)
                        bn(l)
                        if final:
                            dve.wait_ge(l_x, 32)
                        for u in range(UNITS + 1):
                            if u < UNITS:
                                add_bias(l, u)
                            if u >= 1:
                                residual(l, u - 1) if final else low_piece(l, u - 1)
                    layer(0, False)
                    with dve.Fori(1, LAYERS - 1) as l:
                        layer(l, False)
                    layer(LAYERS - 1, True)


def kernel(x, src, dst, edge_attr_16, L0_gnn_W1, L0_gnn_B1, L0_gnn_BNW, L0_gnn_BNB, L0_gnn_W2, L0_gnn_B2,
           L0_gnn_EW, L0_gnn_EB):
    import numpy as np
    import concourse.bacc as bacc
    from concourse.bass_utils import run_bass_kernel_spmd

    def by_tile(a, fill, own=None):
        a = np.asarray(a)
        pad = np.full((PAD_TILES * P,) + a.shape[1:], fill, a.dtype)
        pad[:N_EDGES] = a
        if own is not None:
            pad[SELF_TILE * P:SELF_TILE * P + N_NODES] = own
        return np.ascontiguousarray(np.moveaxis(pad.reshape((PAD_TILES, P) + a.shape[1:]), 1, 0))

    rec = np.ones((N_EDGES, REC), np.float32)
    rec[:, 1:] = np.asarray(edge_attr_16)
    attr = by_tile(rec, 0).reshape(P, PAD_TILES * REC)

    w1, w2 = np.asarray(L0_gnn_W1), np.asarray(L0_gnn_W2)
    ew, eb = np.asarray(L0_gnn_EW), np.asarray(L0_gnn_EB)
    wpack = np.zeros((LAYERS, P, WP_COLS), np.float32)
    wpack[:, :, W1A:W1A + HID] = w1[:, :, :D].transpose(0, 2, 1)
    wpack[:, :, W2T:W2T + HID] = w2.transpose(0, 2, 1).reshape(LAYERS, 2, P, D).transpose(0, 2, 1, 3).reshape(LAYERS, P, HID)
    for at, v in ((B1, L0_gnn_B1), (BNW, L0_gnn_BNW), (BNB, L0_gnn_BNB)):
        wpack[:, :, at:at + 2] = np.asarray(v).reshape(LAYERS, 2, P).transpose(0, 2, 1)
    wpack[:, :, B2:B2 + D] = np.asarray(L0_gnn_B2)[:, None, :]
    mpack = np.zeros((LAYERS, P, MP_COLS), np.float32)
    mpack[:, :, W1B:W1B + HID] = w1[:, :, D:].transpose(0, 2, 1)
    for t in range(TERMS):
        mpack[:, :, EWB + t * REC] = eb
        mpack[:, :, EWB + t * REC + 1:EWB + (t + 1) * REC] = ew
    consts = np.zeros((P, C_COLS), np.float32)
    for t, (s_piece, m_piece) in enumerate(((0, 0), (0, 1), (0, 2), (1, 0), (1, 1), (2, 0))):
        rows = slice(t * REC, (t + 1) * REC)
        consts[t * REC, PLUS1] = 1.0
        consts[rows, S_A] = -1.0 if s_piece >= 1 else 0.0
        consts[rows, S_B] = -1.0 if s_piece >= 2 else 0.0
        consts[rows, M_A] = -1.0 if m_piece >= 1 else 0.0
        consts[rows, M_B] = -1.0 if m_piece >= 2 else 0.0
        consts[0:REC, STACK + t * REC:STACK + (t + 1) * REC] = np.eye(REC)
    consts[:, EPSC] = EPS

    arrays = {
        "x": np.ascontiguousarray(x), "src": by_tile(src, 0, np.arange(N_NODES)),
        "dst": by_tile(dst, -1, np.arange(N_NODES)), "attr": attr, "consts": consts, "wpack": wpack, "mpack": mpack,
    }
    nc = bacc.Bacc("TRN2", target_bir_lowering=False, num_devices=1)
    ins = [nc.dram_tensor(n, a.shape, mybir.dt.from_np(a.dtype), kind="ExternalInput").ap() for n, a in arrays.items()]
    out = nc.dram_tensor("out", (N_NODES, D), F32, kind="ExternalOutput").ap()

    def scratch(name, shape, dt):
        return nc.dram_tensor(name, shape, dt, kind="Internal").ap()
    gin_program(nc, *ins, out, scratch("keys_dram", (P, PAD_TILES * KREC), F32), scratch("deg_dram", (ROUNDS, RCOLS), F32),
                scratch("window_dram", (P,), I32), scratch("rest_dram", (P, NODE_TILES * COLS), BF16))
    r = run_bass_kernel_spmd(nc, [arrays], core_ids=[0])
    return r.results[0]["out"]
```

```python
import concourse.bass as bass
from concourse import mybir
from contextlib import ExitStack

P = 128
N_NODES, D = 3125, 128
N_EDGES, EDGE_F = 103125, 16
HID = 2 * D
LAYERS = 5
EPS = 1e-5

NODE_TILES = -(-N_NODES // P)
LAST_ROWS = N_NODES - (NODE_TILES - 1) * P
HALF = 8
GROUP = 2 * HALF
GROUPS = -(-N_NODES // GROUP)
COLS = GROUPS * GROUP
HCOLS = NODE_TILES * HALF
HKEY = 256
GKEY = 2 * HKEY
WINDOW = 6
A_TILES, B_FIRST = 4, 1
B_TILES = WINDOW - B_FIRST
EDGE_TILES = -(-N_EDGES // P)
SELF_TILE = EDGE_TILES + WINDOW
BATCH = 4
BATCHES = -(-(SELF_TILE + NODE_TILES) // BATCH)
PAD_TILES = BATCHES * BATCH
REC = 1 + EDGE_F
KREC = 4
UNROLL = 4
RING = 7
PACK = PAD_TILES - WINDOW
ROUNDS = GROUPS // UNROLL
RCOLS = UNROLL * GROUP
EXACT = 256
CHUNKS = 7
CW = COLS // CHUNKS
CROUNDS = ROUNDS // CHUNKS
CGROUPS = CROUNDS * UNROLL
UNITS = -(-NODE_TILES // 4)
UW = 4 * P
TERMS = 6
SK = TERMS * REC
PIECES = 2
LN_SCALE = 1024.0
TOP = 2.0 ** 14

ALU = mybir.AluOpType
ACT = mybir.ActivationFunctionType
F32, BF16, FP16, I32 = mybir.dt.float32, mybir.dt.bfloat16, mybir.dt.float16, mybir.dt.int32
AX = mybir.AxisListType

W1A, W2T, B1, BNW, BNB, B2 = 0, 256, 512, 514, 516, 518
WP_COLS = 646
W1B, EWB = 0, 256
MP_COLS = 256 + SK
PLUS1, S_A, S_B, M_A, M_B, EPSC, ZERO, STACK = 0, 1, 2, 3, 4, 5, 6, 8
C_COLS = STACK + SK
ds = bass.ds


class Steps:

    def __init__(self, engine, sem, base=0):
        self.engine, self.sem, self.base, self.n = engine, sem, base, 0

    def then(self, ins):
        self.n += 1
        ins.then_inc(self.sem, 1)
        self.engine.wait_ge(self.sem, self.base + self.n)


def gin_program(nc, x, src, dst, attr, consts, wpack, mpack, out, keys_dram, window_dram, rest_dram):
    assert GROUPS % UNROLL == 0 and COLS % CHUNKS == 0 and ROUNDS % CHUNKS == 0
    assert CGROUPS % RING == 0 and CGROUPS >= NODE_TILES and CROUNDS >= UNITS
    assert CHUNKS % 2 == 1 and UNITS % 2 == 1 and P % RCOLS == 0
    with ExitStack() as whole:
        def sem(name):
            return whole.enter_context(nc.semaphore(name))

        def sb(ctx, name, shape, dt):
            return ctx.enter_context(nc.sbuf_tensor(name, shape, dt))

        banks = [whole.enter_context(nc.psum_tensor(f"bank{i}", [P, 512], F32)) for i in range(8)]
        adj_t = sb(whole, "adj", [P, NODE_TILES * COLS], BF16)
        adj = adj_t[:, :].rearrange("p (k c) -> p k c", k=NODE_TILES)
        hp_t = sb(whole, "h_pieces", [P, NODE_TILES * PIECES * D], FP16)
        hp = hp_t[:, :].rearrange("p (k s f) -> p k s f", k=NODE_TILES, s=PIECES)
        h1 = sb(whole, "h1", [P, 2, COLS], F32)
        agg0 = h1[:, 1, :]
        s6 = sb(whole, "edge_sums", [SK, COLS], BF16)
        cst = sb(whole, "const_rows", [P, C_COLS], F32)
        wp = sb(whole, "weights", [P, WP_COLS], F32)
        mp = h1[:, 0, COLS - MP_COLS:COLS]
        ident = sb(whole, "ident", [P, P], BF16)
        flag = sb(whole, "flag", [1, 1], I32)

        def units(view, u):
            return view[:, 4 * u:min(4 * u + 4, NODE_TILES)]

        def rest_view(c):
            return h1[:, 0, :].bitcast(BF16)[:, ds(c * (2 * CW), CW)]

        l_c = sem("consts_loaded")
        l_wp = sem("weights_loaded")
        l_mp = sem("edge_weights_loaded")
        hp_done = sem("h_pieces_done")

        with ExitStack() as ctx:
            h1_words = h1[:, 0, :].bitcast(BF16)
            cut16 = [0]

            def carve(n, *shape):
                a = cut16[0]
                cut16[0] += 2 * n
                assert cut16[0] <= 2 * (COLS - MP_COLS)
                return h1_words[:, a:a + 2 * n].rearrange("p (b x) -> p b x", b=2)

            a_oh = carve(HCOLS * A_TILES)
            b_oh = carve(HCOLS * B_TILES)
            lo_oh = carve(P * WINDOW)
            dst_oh = sb(ctx, "dst_onehot", [P, UNROLL, GROUP * WINDOW], F32)
            attr_ring = agg0[:, (CHUNKS - 2) * CW:(CHUNKS - 2) * CW + RING * WINDOW * REC].rearrange(
                "p (s x) -> p s x", s=RING)
            key_ring_t = sb(ctx, "key_ring", [P, RING * WINDOW * KREC], F32)
            key_ring = key_ring_t[:, :].rearrange("p (s x) -> p s x", s=RING)
            rel = sb(ctx, "rel_keys", [P, UNROLL, KREC, WINDOW], BF16)
            away = sb(ctx, "dst_distance", [P, UNROLL, GROUP * WINDOW], BF16)
            group_key = sb(ctx, "group_key", [P, GROUPS], F32)
            iota = sb(ctx, "iota", [P, HCOLS, WINDOW], BF16)
            iota_d = sb(ctx, "iota_d", [P, GROUP, WINDOW], BF16)
            sums = sb(ctx, "sums_ring", [REC, RCOLS], F32)
            st0 = sb(ctx, "stacked_sums", [SK, RCOLS], F32)
            st1 = sb(ctx, "stacked_rest", [SK, RCOLS], F32)
            take = sb(ctx, "stacked_take", [SK, RCOLS], F32)
            piece = sb(ctx, "stacked_piece", [SK, RCOLS], BF16)
            window_row = sb(ctx, "window_row", [1, GROUPS // 2], I32)
            thr = sb(ctx, "thr", [P, 2], F32)
            count = sb(ctx, "count", [P, 2], F32)
            window_f = sb(ctx, "window_f", [P, 2], F32)
            window_i = sb(ctx, "window_i", [P, 1], I32)
            ones = sb(ctx, "ones", [P, 1], F32)
            deg_stat = sb(ctx, "degree_stats", [1, 8], F32)
            missing = sb(ctx, "missing", [1, 1], F32)

            words = adj_t[:, :].bitcast(I32)
            wordsf = adj_t[:, :].bitcast(F32)
            cut = [0]

            row = COLS // 2

            def stage(n, f32=False):
                if cut[0] % row + n > row - D:
                    cut[0] += row - cut[0] % row
                a = cut[0]
                cut[0] += n
                return (wordsf if f32 else words)[:, a:a + n]

            src_i, dst_i = stage(PAD_TILES), stage(PAD_TILES)
            lo_i, group_i, in_group_i, hi_i, half_i, mod_i, or_i, key_i = (stage(PAD_TILES) for _ in range(8))
            keys = h1[:, :, :].rearrange("p h c -> p (h c)")[:, 0:PAD_TILES * KREC].rearrange("p (j c) -> p j c", c=KREC)
            first_i = stage(EDGE_TILES)
            first_f = stage(EDGE_TILES, True)
            less0, less1 = stage(EDGE_TILES, True), stage(EDGE_TILES, True)
            x_st = wordsf.rearrange("p (k c) -> p k c", k=NODE_TILES)[:, :, row - D:]
            ln_stats = stage(NODE_TILES * 6, True).rearrange("p (k s) -> p k s", s=6)
            ln_mv = stage(NODE_TILES * 2, True).rearrange("p (k s) -> p k s", s=2)
            ln_sd, ln_inv = (stage(NODE_TILES, True) for _ in range(2))
            last_row = row * (NODE_TILES - 1)
            ln_rstd = wordsf[:, last_row + row - D - 2 * NODE_TILES:last_row + row - D - NODE_TILES]
            ln_shift = wordsf[:, last_row + row - D - NODE_TILES:last_row + row - D]
            assert cut[0] <= last_row and D + 2 * NODE_TILES <= CW // 2

            s_dst = sem("dst_loaded")
            s_src = sem("src_loaded")
            s_first = sem("firsts_loaded")
            s_x = sem("x_loaded")
            s_zero = sem("x_pad_zeroed")
            s_thr = sem("thresholds_made")
            s_const = sem("constants_made")
            s_chain = sem("dve_chain")
            s_lo = sem("source_in_tile_made")
            s_kact = sem("keys_by_act")
            s_kdve = sem("keys_by_dve")
            s_kst = sem("keys_stored")
            s_count = sem("window_counted")
            s_wd = sem("window_stored")
            s_wr = sem("window_row_loaded")
            s_mv = sem("ln_moments")
            s_sd = sem("ln_deviation")
            s_y = sem("ln_normalised")
            s_hi = sem("ln_high_piece")

            with nc.Block() as block:
                @block.sync
                def _(sp):
                    sp.dma_start(first_i, dst[0:1, 0:EDGE_TILES].partition_broadcast(P)).then_inc(s_first, 16)
                    sp.dma_start(dst_i, dst).then_inc(s_dst, 16)
                    sp.dma_start(cst[:, :], consts).then_inc(l_c, 16)
                    sp.dma_start(wp[:, :], wpack[0]).then_inc(l_wp, 16)
                    sp.wait_ge(s_count, 1)
                    sp.dma_start(window_dram.rearrange("(p h) -> p h", h=1), window_i[:, :]).then_inc(s_wd, 16)
                    sp.wait_ge(s_wd, 16)
                    sp.dma_start(window_row[:, :], window_dram[0:GROUPS // 2].rearrange("(a n) -> a n", a=1)).then_inc(s_wr, 16)
                    sp.wait_ge(s_kact, 1)
                    sp.wait_ge(s_kdve, 1)
                    sp.dma_start(keys_dram, keys.rearrange("p j c -> p (j c)")).then_inc(s_kst, 16)
                    sp.wait_ge(s_wr, 16)
                    sp.wait_ge(s_kst, 16)

                @block.scalar
                def _(act):
                    act.dma_start(src_i, src).then_inc(s_src, 16)
                    act.dma_start(x_st[:, 0:NODE_TILES - 1, :],
                                  x[0:(NODE_TILES - 1) * P, :].rearrange("(k p) f -> p k f", p=P)).then_inc(s_x, 16)
                    act.wait_ge(s_zero, 1)
                    act.dma_start(x_st[0:LAST_ROWS, NODE_TILES - 1, :],
                                  x[(NODE_TILES - 1) * P:N_NODES, :]).then_inc(s_x, 16)
                    act.wait_ge(s_dst, 16)
                    nc.scalar.activation(keys[:, :, 2], dst_i, ACT.Copy, scale=float(GKEY // GROUP))
                    act.wait_ge(s_lo, 1)
                    nc.scalar.activation(keys[:, :, 3], in_group_i, ACT.Copy).then_inc(s_kact, 1)
                    act.wait_ge(s_mv, 1)
                    act.wait_ge(l_c, 16)
                    nc.scalar.activation(ln_sd, ln_mv[:, :, 1], ACT.Sqrt, bias=cst[:, EPSC:EPSC + 1]).then_inc(s_sd, 1)

                @block.gpsimd
                def _(pool):
                    nc.gpsimd.memset(x_st[:, NODE_TILES - 1, :], 0.0).then_inc(s_zero, 1)
                    nc.gpsimd.iota(thr[:, :], [[GROUP, 2]], base=0, channel_multiplier=2 * GROUP,
                                   allow_small_or_imprecise_dtypes=True).then_inc(s_thr, 1)
                    nc.gpsimd.memset(ident[:, :], 0.0).then_inc(s_zero, 1)
                    nc.gpsimd.memset(ones[:, :], 1.0)
                    nc.gpsimd.iota(group_key[:, :], [[GKEY, GROUPS]], base=0, channel_multiplier=0,
                                   allow_small_or_imprecise_dtypes=True)
                    nc.gpsimd.iota(iota[:, :, :], [[1, HCOLS], [0, WINDOW]], base=0, channel_multiplier=0,
                                   allow_small_or_imprecise_dtypes=True)
                    nc.gpsimd.iota(iota_d[:, :, :], [[GKEY // GROUP, GROUP], [0, WINDOW]], base=0, channel_multiplier=0,
                                   allow_small_or_imprecise_dtypes=True)
                    pool.wait_ge(s_zero, 2)
                    nc.gpsimd.affine_select(out=ident[:, :], in_=ident[:, :], compare_op=ALU.not_equal, fill=1.0,
                                            base=0, pattern=[[-1, P]], channel_multiplier=1).then_inc(s_const, 1)
                    pool.wait_ge(s_const, 1)

                @block.vector
                def _(dve):
                    V = nc.vector
                    steps = Steps(dve, s_chain)
                    dve.wait_ge(s_first, 16)
                    steps.then(V.tensor_copy(first_f, first_i))
                    dve.wait_ge(s_thr, 1)
                    V.tensor_scalar(less0, first_f, thr[:, 0:1], None, ALU.is_lt, ALU.add, accum_out=count[:, 0:1])
                    steps.then(V.tensor_scalar(less1, first_f, thr[:, 1:2], None, ALU.is_lt, ALU.add,
                                               accum_out=count[:, 1:2]))
                    steps.then(V.tensor_scalar(window_f[:, :], count[:, :], -1.0, 0.0, ALU.add, ALU.max))
                    V.scalar_tensor_tensor(window_i[:, :], window_f[:, 1:2], float(PACK), window_f[:, 0:1], ALU.mult,
                                           ALU.add).then_inc(s_count, 1)
                    dve.wait_ge(s_src, 16)
                    dve.wait_ge(s_dst, 16)
                    V.tensor_scalar(lo_i, src_i, P - 1, None, ALU.bitwise_and)
                    steps.then(V.tensor_scalar(group_i, dst_i, 4, 9, ALU.arith_shift_right, ALU.logical_shift_left))
                    V.tensor_tensor(in_group_i, lo_i, group_i, ALU.bitwise_or).then_inc(s_lo, 1)
                    V.tensor_scalar(hi_i, src_i, 7, 3, ALU.logical_shift_right, ALU.logical_shift_left)
                    V.tensor_scalar(half_i, dst_i, 3, 8, ALU.arith_shift_right, ALU.logical_shift_left)
                    steps.then(V.tensor_scalar(mod_i, dst_i, HALF - 1, None, ALU.bitwise_and))
                    steps.then(V.tensor_tensor(or_i, half_i, mod_i, ALU.bitwise_or))
                    steps.then(V.tensor_tensor(key_i, or_i, hi_i, ALU.bitwise_or))
                    V.tensor_copy(keys[:, :, 0], key_i)
                    V.tensor_scalar(keys[:, :, 1], key_i, -float(HKEY), None, ALU.add).then_inc(s_kdve, 1)
                    dve.wait_ge(s_x, 32)
                    dve.wait_ge(s_zero, 1)
                    for k in range(NODE_TILES):
                        last = V.bn_stats(ln_stats[:, k, :], x_st[:, k, :])
                    steps.then(last)
                    for k in range(NODE_TILES):
                        last = V.bn_aggr(ln_mv[:, k, :], ln_stats[:, k, :])
                    last.then_inc(s_mv, 1)
                    dve.wait_ge(s_sd, 1)
                    steps.then(V.reciprocal(ln_inv, ln_sd))
                    steps.then(V.tensor_scalar(ln_rstd, ln_inv, LN_SCALE, None, ALU.mult))
                    steps.then(V.scalar_tensor_tensor(ln_shift, ln_mv[:, :, 0], -1.0, ln_rstd, ALU.mult,
                                                      ALU.mult))

            s_away = sem("dst_distance_made")
            s_sq = sem("dst_distance_squared")
            s_dst_oh = sem("dst_onehot_made")
            s_key = [sem(f"key_window_loaded{i}") for i in range(RING)]
            s_attr = [sem(f"attr_window_loaded{i}") for i in range(RING)]
            s_rel = sem("rel_keys_made")
            s_oh = sem("onehots_made")
            s_a_used = sem("first_half_counted")
            s_b_used = sem("both_halves_counted")
            s_cnt = sem("group_counted")
            s_ev = sem("group_evacuated")
            s_stack = sem("sums_stacked")
            s_st0 = sem("stacked_sums_out")
            s_own = sem("own_edges_added")
            s_pc = sem("pool_chain")
            s_s6 = sem("edge_sum_pieces")
            s_agg0 = sem("first_layer_chunk")
            s_agg0_ev = sem("first_layer_chunk_out")
            cnt_ps, att_ps, stack_ps, agg0_ps = banks[0:2], banks[2:4], banks[4], banks[5]
            CHAIN = 4

            def h_view(t, j):
                return t.rearrange("p (c j) -> p c j", j=j)

            def count_products(b, u, slot, tiles, first, used=None):
                na, nb, b0, wl = (A_TILES, B_TILES, B_FIRST, WINDOW) if tiles is None else (tiles, tiles, 0, tiles)
                av = h_view(a_oh[:, b, 0:HCOLS * na], na)
                bv = h_view(b_oh[:, b, 0:HCOLS * nb], nb)
                lv = h_view(lo_oh[:, b, 0:P * wl], wl)
                dv = h_view(dst_oh[:, u, 0:GROUP * wl], wl)
                for j in range(na):
                    last = nc.tensor.matmul(cnt_ps[b][:, 0:HCOLS], lv[:, :, j], av[:, :, j], start=(first and j == 0),
                                     stop=(j == na - 1), skip_group_check=True)
                if used is not None:
                    last.then_inc(used[0], 1)
                for j in range(nb):
                    last = nc.tensor.matmul(cnt_ps[b][:, HCOLS:2 * HCOLS], lv[:, :, b0 + j], bv[:, :, j], start=False,
                                     stop=(j == nb - 1), skip_group_check=True)
                if used is not None:
                    last.then_inc(used[1], 1)
                for j in range(wl):
                    last = nc.tensor.matmul(att_ps[b][0:REC, 0:GROUP], attr_ring[:, slot, j * REC:(j + 1) * REC],
                                            dv[:, :, j], start=(first and j == 0), stop=(j == wl - 1),
                                            skip_group_check=True)
                return last

            def one_hots(b, u, tiles, second=None):
                na, nb, b0, wl = (A_TILES, B_TILES, B_FIRST, WINDOW) if tiles is None else (tiles, tiles, 0, tiles)

                def equal(out, values, key, n, j):
                    return nc.vector.tensor_tensor(h_view(out, j), values[:, 0:n, 0:j],
                                                   key.unsqueeze(1).to_broadcast([P, n, j]), ALU.is_equal)
                equal(a_oh[:, b, 0:HCOLS * na], iota, rel[:, u, 0, 0:na], HCOLS, na)
                if second is not None:
                    second()
                equal(b_oh[:, b, 0:HCOLS * nb], iota, rel[:, u, 1, b0:b0 + nb], HCOLS, nb)
                return equal(lo_oh[:, b, 0:P * wl], iota, rel[:, u, 3, 0:wl], P, wl)

            def dst_one_hot(engine, b, u, wl):
                return engine.tensor_tensor(h_view(dst_oh[:, b, 0:GROUP * wl], wl), iota_d[:, :, 0:wl],
                                            rel[:, u, 2, 0:wl].unsqueeze(1).to_broadcast([P, GROUP, wl]), ALU.is_equal)

            def relative(slot, u, g, wl):
                rec = key_ring[:, slot, 0:wl * KREC].rearrange("p (j c) -> p c j", c=KREC)
                return nc.gpsimd.tensor_tensor(rel[:, u, :, 0:wl], rec,
                                               group_key[:, ds(g, 1)].unsqueeze(1).to_broadcast([P, KREC, wl]),
                                               ALU.subtract)

            def out_view(g):
                return adj[:, :, ds(g * GROUP, GROUP)].rearrange("p k (s m) -> p s k m", s=2)

            def bank_view(b):
                return cnt_ps[b][:, 0:2 * HCOLS].rearrange("p (s k m) -> p s k m", s=2, m=HALF)

            def sum_pieces(steps, col, w):
                G = nc.gpsimd

                def column(c):
                    return cst[0:SK, c:c + 1].to_broadcast([SK, w])
                steps.then(G.tensor_tensor(take[:, 0:w], piece[:, 0:w], column(S_A), ALU.mult))
                steps.then(G.tensor_tensor(st1[:, 0:w], st0[:, 0:w], take[:, 0:w], ALU.add))
                steps.then(G.tensor_tensor(piece[:, 0:w], st1[:, 0:w], column(ZERO), ALU.add))
                steps.then(G.tensor_tensor(take[:, 0:w], piece[:, 0:w], column(S_B), ALU.mult))
                return G.tensor_tensor(s6[:, ds(col, w)], st1[:, 0:w], take[:, 0:w], ALU.add)

            def agg0_products(k, c, stop):
                for s in range(PIECES):
                    last = nc.tensor.matmul(agg0_ps[:, 0:CW], hp[:, k, s, :], adj[:, k, ds(c * CW, CW)],
                                            start=(k == 0 and s == 0), stop=stop and s == PIECES - 1)
                return last

            def stack_round(pe, r):
                pe.wait_ge(s_ev, (r + 1) * UNROLL)
                nc.tensor.matmul(stack_ps[0:SK, 0:RCOLS], cst[0:REC, STACK:STACK + SK], sums[:, :],
                                 start=True, stop=True).then_inc(s_stack, 1)

            def stacked_out(w):
                for out in (st0, piece):
                    last = nc.scalar.activation(out[:, 0:w], stack_ps[0:SK, 0:w], ACT.Identity,
                                                bias=cst[0:SK, PLUS1:PLUS1 + 1])
                return last

            def evac_stack(act, r, first):
                act.wait_ge(s_stack, r + 1)
                if not first:
                    act.wait_ge(s_s6, r)
                stacked_out(RCOLS).then_inc(s_st0, 1)

            def add_own(pool, r):
                pool.wait_ge(s_ev, (r + 1) * UNROLL)
                half = r % (P // RCOLS)
                col = r // (P // RCOLS) * COLS + r * RCOLS
                own = adj_t[:, ds(col, RCOLS)]
                nc.gpsimd.tensor_tensor(own, own, ident[:, ds(half * RCOLS, RCOLS)], ALU.add).then_inc(s_own, 1)

            def round_pieces(pool, r):
                pool.wait_ge(s_st0, r + 1)
                steps = Steps(pool, s_pc, r * CHAIN)
                sum_pieces(steps, r * RCOLS, RCOLS).then_inc(s_s6, 1)
                assert steps.n == CHAIN

            with nc.Block() as block:
                @block.sync
                def _(sp):
                    def load_rings(t, first):
                        for q in range(RING):
                            pair = sp.value_load(window_row[0:1, ds(t * RING + q, 1)], min_val=0,
                                                 max_val=(EDGE_TILES - 1) * (PACK + 1))
                            for i, start in ((2 * q, pair % PACK), (2 * q + 1, pair // PACK)):
                                if not (first and i < RING):
                                    sp.wait_ge(s_cnt, t * (2 * RING) - RING + i + 1)
                                slot = i % RING
                                sp.dma_start(key_ring[:, slot, :].rearrange("p (j c) -> p j c", c=KREC),
                                             keys_dram.rearrange("p (j c) -> p j c", c=KREC)[:, ds(start, WINDOW), :]
                                             ).then_inc(s_key[slot], 16)
                                sp.dma_start(attr_ring[:, slot, :].rearrange("p (j c) -> p j c", c=REC),
                                             attr.rearrange("p (j c) -> p j c", c=REC)[:, ds(start, WINDOW), :]
                                             ).then_inc(s_attr[slot], 16)
                    load_rings(0, True)
                    with sp.Fori(1, GROUPS // (2 * RING)) as t:
                        load_rings(t, False)

                @block.gpsimd
                def _(pool):
                    def keys(c, i):
                        pool.wait_ge(s_key[i % RING], (c * (CGROUPS // RING) + i // RING + 1) * 16)
                        u = i % UNROLL
                        relative(i % RING, u, c * CGROUPS + i, WINDOW).then_inc(s_rel, 1)
                        pool.wait_ge(s_rel, c * CGROUPS + i + 1)
                        nc.gpsimd.tensor_tensor(h_view(away[:, u, :], WINDOW), iota_d[:, :, :],
                                                rel[:, u, 2, :].unsqueeze(1).to_broadcast([P, GROUP, WINDOW]),
                                                ALU.subtract).then_inc(s_away, 1)

                    def low_piece(u):
                        pool.wait_ge(s_hi, u + 1)
                        nc.gpsimd.tensor_tensor(units(hp, u)[:, :, 1, :], units(x_st, u), units(hp, u)[:, :, 0, :],
                                                ALU.subtract).then_inc(hp_done, 1)

                    def chunk(c, first, last):
                        for i in range(CGROUPS):
                            g = c * CGROUPS + i
                            if not (first and i < 2):
                                pool.wait_ge(s_oh, g - 1)
                                pool.wait_ge(s_dst_oh, g - 1)
                            if not (last and i >= CGROUPS - 2):
                                keys(c, i + 2)
                            if i % UNROLL == UNROLL - 1 and not (first and i < UNROLL):
                                add_own(pool, c * CROUNDS + i // UNROLL - 1)
                            if i % UNROLL == 0 and not (first and i < 2 * UNROLL):
                                round_pieces(pool, c * CROUNDS + i // UNROLL - 2)
                            if first and i % UNROLL == UNROLL - 1 and 1 <= i // UNROLL < UNITS:
                                low_piece(i // UNROLL - 1)
                        if first:
                            low_piece(UNITS - 1)
                    keys(0, 0)
                    keys(0, 1)
                    chunk(0, True, False)
                    with pool.Fori(1, CHUNKS - 1) as c:
                        chunk(c, False, False)
                    chunk(CHUNKS - 1, False, True)
                    round_pieces(pool, ROUNDS - 2)

                @block.vector
                def _(dve):
                    def round_(r, first):
                        for u in range(UNROLL):
                            g = r * UNROLL + u
                            dve.wait_ge(s_rel, g + 1)
                            again = not (first and u < 2)
                            if again:
                                dve.wait_ge(s_a_used, g - 1)

                            def second():
                                if again:
                                    dve.wait_ge(s_b_used, g - 1)
                            one_hots(u % 2, u, None, second).then_inc(s_oh, 1)
                    round_(0, True)
                    with dve.Fori(1, ROUNDS) as r:
                        round_(r, False)

                @block.tensor
                def _(pe):
                    def chunk(c, first):
                        for i in range(CGROUPS):
                            u = i % UNROLL
                            r = c * CROUNDS + i // UNROLL
                            g = r * UNROLL + u
                            b, slot = u % 2, i % RING
                            pe.wait_ge(s_oh, g + 1)
                            pe.wait_ge(s_dst_oh, g + 1)
                            pe.wait_ge(s_attr[slot], (c * (CGROUPS // RING) + i // RING + 1) * 16)
                            if not (first and i < 2):
                                pe.wait_ge(s_ev, g - 1)
                            count_products(b, u, slot, None, True, (s_a_used, s_b_used)).then_inc(s_cnt, 1)
                            if u == 0 and not (first and i == 0):
                                stack_round(pe, r - 1)
                            k = i - (CGROUPS - NODE_TILES)
                            if not first and k >= 0:
                                if k == 0:
                                    pe.wait_ge(s_own, c * CROUNDS)
                                    pe.wait_ge(hp_done, UNITS)
                                last = agg0_products(k, c - 1, k == NODE_TILES - 1)
                                if k == NODE_TILES - 1:
                                    last.then_inc(s_agg0, 1)
                    chunk(0, True)
                    with pe.Fori(1, CHUNKS) as c:
                        chunk(c, False)

                @block.scalar
                def _(act):
                    def normalise(k):
                        nc.scalar.activation(x_st[:, k, :], x_st[:, k, :], ACT.Relu, bias=ln_shift[:, k:k + 1],
                                             scale=ln_rstd[:, k:k + 1]).then_inc(s_y, 1)

                    def dst_one_hot_(g, u):
                        act.wait_ge(s_away, g + 1)
                        nc.scalar.activation(away[:, u, :], away[:, u, :], ACT.Square).then_inc(s_sq, 1)
                        act.wait_ge(s_sq, g + 1)
                        nc.scalar.activation(dst_oh[:, u, :], away[:, u, :], ACT.Relu, bias=ones[:, 0:1],
                                             scale=-1.0).then_inc(s_dst_oh, 1)

                    LEAD = 2

                    def round_(r, chunk0, last_round=False):
                        for u in range(UNROLL):
                            g = r * UNROLL + u
                            act.wait_ge(s_cnt, g + 1)
                            nc.scalar.activation(out_view(g), bank_view(u % 2), ACT.Copy)
                            if u == 0 and not (chunk0 and r == 0):
                                act.wait_ge(s_stack, r)
                            nc.scalar.activation(sums[:, u * GROUP:(u + 1) * GROUP], att_ps[u % 2][0:REC, 0:GROUP],
                                                 ACT.Copy).then_inc(s_ev, 1)
                            if u == 0 and not (chunk0 and r == 0):
                                evac_stack(act, r - 1, chunk0 and r == 1)
                            if not (last_round and u + LEAD >= UNROLL):
                                dst_one_hot_(g + LEAD, (u + LEAD) % UNROLL)
                            if chunk0 and g < NODE_TILES:
                                normalise(g)
                        if chunk0 and r < UNITS:
                            act.wait_ge(s_y, min((r + 1) * 4, NODE_TILES))
                            nc.scalar.activation(units(hp, r)[:, :, 0, :], units(x_st, r), ACT.Copy).then_inc(s_hi, 1)
                    def chunk_out(c):
                        act.wait_ge(s_agg0, c)
                        nc.scalar.activation(agg0[:, ds((c - 1) * CW, CW)], agg0_ps[:, 0:CW], ACT.Copy).then_inc(s_agg0_ev, 1)
                    for u in range(LEAD):
                        dst_one_hot_(u, u)
                    for r in range(CROUNDS):
                        round_(r, True)
                    with act.Fori(1, CHUNKS - 1) as c:
                        with act.Fori(0, CROUNDS) as q:
                            round_(c * CROUNDS + q, False)
                        chunk_out(c)
                    with act.Fori((CHUNKS - 1) * CROUNDS, ROUNDS - 1) as r:
                        round_(r, False)
                    round_(ROUNDS - 1, False, True)
                    chunk_out(CHUNKS - 1)

            s_flag = sem("flag_chain")
            with nc.Block() as block:
                @block.sync
                def _(sp):
                    sp.dma_start(mp, mpack[0]).then_inc(l_mp, 16)

                @block.tensor
                def _(pe):
                    stack_round(pe, ROUNDS - 1)
                    pe.wait_ge(s_own, ROUNDS)
                    pe.wait_ge(s_agg0_ev, CHUNKS - 1)
                    for k in range(NODE_TILES):
                        last = agg0_products(k, CHUNKS - 1, k == NODE_TILES - 1)
                    last.then_inc(s_agg0, 1)

                @block.gpsimd
                def _(pool):
                    add_own(pool, ROUNDS - 1)
                    round_pieces(pool, ROUNDS - 1)
                    pool.wait_ge(s_s6, ROUNDS)

                @block.scalar
                def _(act):
                    evac_stack(act, ROUNDS - 1, False)
                    act.wait_ge(s_agg0, CHUNKS)
                    nc.scalar.activation(agg0[:, (CHUNKS - 1) * CW:COLS], agg0_ps[:, 0:CW], ACT.Copy).then_inc(s_agg0_ev, 1)
                    act.wait_ge(s_agg0_ev, CHUNKS)

                @block.vector
                def _(dve):
                    V = nc.vector
                    steps = Steps(dve, s_flag)
                    done = (ROUNDS - 1) * RCOLS
                    for rounds, at, a, b in ((ROUNDS - 1, 0, 0, done), (ROUNDS, 2, done, COLS)):
                        dve.wait_ge(s_s6, rounds)
                        V.tensor_reduce(deg_stat[:, at:at + 1], s6[0:1, a:b], AX.X, ALU.add)
                        steps.then(V.tensor_reduce(deg_stat[:, at + 1:at + 2], s6[0:1, a:b], AX.X, ALU.max))
                    V.tensor_tensor(deg_stat[:, 4:5], deg_stat[:, 0:1], deg_stat[:, 2:3], ALU.add)
                    steps.then(V.tensor_tensor(deg_stat[:, 5:6], deg_stat[:, 1:2], deg_stat[:, 3:4], ALU.max))
                    V.tensor_scalar(deg_stat[:, 6:7], deg_stat[:, 4:5], float(N_EDGES + COLS), None, ALU.not_equal)
                    steps.then(V.tensor_scalar(deg_stat[:, 7:8], deg_stat[:, 5:6], float(EXACT), None, ALU.is_ge))
                    steps.then(V.tensor_tensor(missing[:, :], deg_stat[:, 6:7], deg_stat[:, 7:8], ALU.add))
                    steps.then(V.tensor_scalar(flag[:, :], missing[:, :], 0.5, None, ALU.is_ge))

            general = nc.values_load(flag[0:1, 0:1], min_val=0, max_val=1)
            rest = a_oh[:, 1, 0:2 * HCOLS]
            s_gw = sem("general_window_loaded")
            s_grel = sem("general_rel_keys_made")
            s_goh = sem("general_onehots_made")
            s_gcnt = sem("general_batch_counted")
            s_gev = sem("general_group_evacuated")
            s_grest = sem("general_rest_made")
            s_gst = sem("general_rest_stored")
            s_gstack = sem("general_sums_stacked")
            s_gst0 = sem("general_stacked_sums_out")
            s_gpc = sem("general_pool_chain")
            s_gs6 = sem("general_edge_sum_pieces")
            s_gload = sem("general_rest_loaded")
            s_gfree = sem("general_rest_buffer_free")
            s_gagg = sem("general_chunk")
            s_gagg_ev = sem("general_chunk_out")
            with nc.If(general > 0):
                with nc.Block() as block:
                    @block.sync
                    def _(sp):
                        def load(t):
                            sp.dma_start(key_ring[:, 0, 0:BATCH * KREC], keys_dram[:, ds(t * (BATCH * KREC), BATCH * KREC)]
                                         ).then_inc(s_gw, 16)
                            sp.dma_start(attr_ring[:, 0, 0:BATCH * REC], attr[:, ds(t * (BATCH * REC), BATCH * REC)]
                                         ).then_inc(s_gw, 16)
                        with sp.Fori(0, GROUPS) as g:
                            load(0)
                            with sp.Fori(1, BATCHES) as t:
                                sp.wait_ge(s_gcnt, g * BATCHES + t)
                                load(t)
                            sp.wait_ge(s_grest, g + 1)
                            for s in range(2):
                                sp.dma_start(rest_dram.rearrange("p (k c) -> p k c", k=NODE_TILES)
                                             [:, :, ds(g * GROUP + s * HALF, HALF)],
                                             rest[:, s * HCOLS:(s + 1) * HCOLS].rearrange("p (k m) -> p k m", m=HALF)
                                             ).then_inc(s_gst, 16)
                        sp.wait_ge(s_gst, 32 * GROUPS)
                        with sp.Fori(0, CHUNKS) as c:
                            with sp.Fori(0, NODE_TILES) as k:
                                sp.wait_ge(s_gfree, c * NODE_TILES + k + 1)
                                sp.dma_start(rest_view(0), rest_dram[:, ds(k * COLS + c * CW, CW)]).then_inc(s_gload, 16)

                    @block.gpsimd
                    def _(pool):
                        with pool.Fori(0, GROUPS) as g:
                            with pool.Fori(0, BATCHES) as t:
                                pool.wait_ge(s_gw, (g * BATCHES + t + 1) * 32)
                                relative(0, 0, g, BATCH).then_inc(s_grel, 1)
                                pool.wait_ge(s_goh, g * BATCHES + t + 1)
                            pool.wait_ge(s_gst0, g + 1)
                            steps = Steps(pool, s_gpc, g * CHAIN)
                            sum_pieces(steps, g * GROUP, GROUP).then_inc(s_gs6, 1)

                    @block.vector
                    def _(dve):
                        with dve.Fori(0, GROUPS) as g:
                            with dve.Fori(0, BATCHES) as t:
                                dve.wait_ge(s_grel, g * BATCHES + t + 1)
                                one_hots(0, 0, BATCH)
                                dst_one_hot(nc.vector, 0, 0, BATCH).then_inc(s_goh, 1)
                                dve.wait_ge(s_gcnt, g * BATCHES + t + 1)
                            dve.wait_ge(s_gev, g + 1)
                            for s in range(2):
                                last = nc.vector.tensor_tensor(
                                    rest[:, s * HCOLS:(s + 1) * HCOLS].rearrange("p (k m) -> p k m", m=HALF),
                                    bank_view(0)[:, s], out_view(g)[:, s], ALU.subtract)
                            last.then_inc(s_grest, 1)
                            dve.wait_ge(s_gst, (g + 1) * 32)

                    @block.tensor
                    def _(pe):
                        def batch(g, t, first):
                            pe.wait_ge(s_goh, g * BATCHES + t + 1)
                            count_products(0, 0, 0, BATCH, first).then_inc(s_gcnt, 1)
                        with pe.Fori(0, GROUPS) as g:
                            batch(g, 0, True)
                            with pe.Fori(1, BATCHES) as t:
                                batch(g, t, False)
                            pe.wait_ge(s_gev, g + 1)
                            nc.tensor.matmul(stack_ps[0:SK, 0:GROUP], cst[0:REC, STACK:STACK + SK], sums[:, 0:GROUP],
                                             start=True, stop=True).then_inc(s_gstack, 1)
                            pe.wait_ge(s_grest, g + 1)
                            pe.wait_ge(s_gst0, g + 1)
                        pe.sem_inc(s_gfree, 1)
                        with pe.Fori(0, CHUNKS) as c:
                            for k in range(NODE_TILES):
                                agg0_products(k, c, False)
                            for k in range(NODE_TILES):
                                pe.wait_ge(s_gload, (c * NODE_TILES + k + 1) * 16)
                                for s in range(PIECES):
                                    last = nc.tensor.matmul(agg0_ps[:, 0:CW], hp[:, k, s, :], rest_view(0), start=False,
                                                            stop=(k == NODE_TILES - 1 and s == PIECES - 1))
                                last.then_inc(s_gfree, 1)
                            pe.wait_ge(s_gfree, (c + 1) * NODE_TILES + 1)
                            nc.tensor.sem_inc(s_gagg, 1)
                            pe.wait_ge(s_gagg_ev, c + 1)

                    @block.scalar
                    def _(act):
                        with act.Fori(0, GROUPS) as g:
                            act.wait_ge(s_gcnt, (g + 1) * BATCHES)
                            nc.scalar.activation(out_view(g), bank_view(0), ACT.Copy)
                            nc.scalar.activation(sums[:, 0:GROUP], att_ps[0][0:REC, 0:GROUP], ACT.Copy
                                                 ).then_inc(s_gev, 1)
                            act.wait_ge(s_gstack, g + 1)
                            stacked_out(GROUP).then_inc(s_gst0, 1)
                        with act.Fori(0, CHUNKS) as c:
                            act.wait_ge(s_gagg, c + 1)
                            nc.scalar.activation(agg0[:, ds(c * CW, CW)], agg0_ps[:, 0:CW], ACT.Copy).then_inc(s_gagg_ev, 1)

        with ExitStack() as ctx:
            aggT = sb(ctx, "aggT", [P, max(CW, 2 * D)], F32)
            m6 = sb(ctx, "edge_weights", [SK, HID], BF16)
            mt = sb(ctx, "edge_weights_f", [SK, HID], F32)
            uw = sb(ctx, "bound_parts", [P, HID], F32)
            row = sb(ctx, "bound_row", [P, 4, D], F32)
            ones = sb(ctx, "ones2", [P, P], F32)
            inv = sb(ctx, "inverse_scale", [P, 1], F32)
            stats = sb(ctx, "bn_stats", [P, 2, CHUNKS * 6], F32)
            small = sb(ctx, "bn_small", [P, 22], F32)
            mv = small[:, 0:4].rearrange("p (h s) -> p h s", h=2)
            ab = small[:, 4:8]
            mean_b, sd, rstd, scale, shift, ms, ub = (small[:, a:a + 2] for a in range(8, 22, 2))
            x_res = hp_t[:, 0:2 * NODE_TILES * D].bitcast(F32).rearrange("p (k f) -> p k f", k=NODE_TILES)

            agg_ps, w2_ps = banks[0:2], banks[2:4]
            w1_ps = [banks[4:6], banks[6:8]]

            l_x = sem("residual_loaded")
            rest_loaded = sem("count_rest_loaded")
            rest_free = sem("count_rest_buffer_free")
            ones_done = sem("ones_made")
            m_ps = sem("edge_weights_product")
            m_done = sem("edge_weight_pieces")
            w_chain = sem("weights_chain")
            w1_scaled = sem("w1_scaled")
            uw_done = sem("bound_parts_done")
            bound = sem("bound_summed")
            w2_scaled = sem("w2_scaled")
            agg_done = sem("agg_done")
            agg_ev = sem("agg_evacuated")
            w1_done = sem("w1_done")
            h1_ev = sem("h1_evacuated")
            st_done = sem("bn_stats_done")
            st_last = sem("bn_stats_complete")
            mv_done = sem("bn_moments_done")
            sd_done = sem("bn_deviation_done")
            relu0_done = sem("first_unit_second_half_done")
            bn_c = sem("bn_chain")
            bn_ready = sem("bn_ready")
            relu_done = sem("relu_done")
            w2_done = sem("w2_done")
            t_done = sem("bias_added")
            hi_done = sem("high_piece_done")
            o_done = sem("out_added")
            o_st = sem("out_stored")
            BN_STEPS = 4
            WSTEPS = 16

            def tiles_of(u):
                return 1 if u == UNITS - 1 else 4

            def rows_of(u):
                return LAST_ROWS if u == UNITS - 1 else P

            def unit_view(half, u):
                k, r = tiles_of(u), rows_of(u)
                if u == UNITS - 1:
                    return aggT[0:r, half * D:(half + 1) * D].rearrange("p (k f) -> p k f", k=k)
                return h1[0:r, half, u * UW:u * UW + k * P].rearrange("p (k f) -> p k f", k=k)

            def w2_view(u):
                k, r = tiles_of(u), rows_of(u)
                return w2_ps[u % 2][0:r, 0:k * P].rearrange("p (k f) -> p k f", k=k)

            def hp_view(u, piece):
                k, r = tiles_of(u), rows_of(u)
                return hp[0:r, u * 4:u * 4 + k, piece, :]

            def later(l):
                return not (isinstance(l, int) and l == 0)

            with nc.Block() as block:
                @block.sync
                def _(sp):
                    def load_layer(l):
                        sp.wait_ge(hp_done, (l + 1) * UNITS)
                        sp.dma_start(mp, mpack[ds(l, 1)].rearrange("a p c -> (a p) c")).then_inc(l_mp, 16)
                        sp.dma_start(wp[:, :], wpack[ds(l, 1)].rearrange("a p c -> (a p) c")).then_inc(l_wp, 16)
                        with sp.If(general > 0):
                            with sp.Fori(0, CHUNKS) as c:
                                with sp.Fori(0, NODE_TILES) as k:
                                    sp.wait_ge(rest_free, ((l - 1) * CHUNKS + c) * NODE_TILES + k + 1)
                                    sp.dma_start(rest_view(c), rest_dram[:, ds(k * COLS + c * CW, CW)]
                                                 ).then_inc(rest_loaded, 16)
                    with sp.Fori(1, LAYERS) as l:
                        load_layer(l)
                    sp.wait_ge(agg_done, (LAYERS - 1) * CHUNKS)
                    sp.dma_start(x_res[:, 0:NODE_TILES - 1, :],
                                 x[0:(NODE_TILES - 1) * P, :].rearrange("(k p) f -> p k f", p=P)).then_inc(l_x, 16)
                    sp.dma_start(x_res[0:LAST_ROWS, NODE_TILES - 1, :],
                                 x[(NODE_TILES - 1) * P:N_NODES, :]).then_inc(l_x, 16)
                    for u in range(UNITS):
                        sp.wait_ge(o_done, u + 1)
                        if u < UNITS - 1:
                            sp.dma_start(out[u * UW:(u + 1) * UW, :].rearrange("(k p) f -> p k f", p=P),
                                         unit_view(1, u)).then_inc(o_st, 16)
                        else:
                            sp.dma_start(out[u * UW:N_NODES, :], aggT[0:LAST_ROWS, D:2 * D]).then_inc(o_st, 16)
                    sp.wait_ge(o_st, 16 * UNITS)

                @block.tensor
                def _(pe):
                    def aggregate(l, c, b):
                        n = (l - 1) * CHUNKS + c
                        if not (isinstance(c, int) and c < 2):
                            pe.wait_ge(agg_ev, n - 1)

                        def products(k, stop):
                            for s in range(PIECES):
                                last = nc.tensor.matmul(agg_ps[b][:, 0:CW], hp[:, k, s, :], adj[:, k, ds(c * CW, CW)],
                                                        start=(k == 0 and s == 0), stop=stop and s == PIECES - 1)
                            return last
                        for k in range(NODE_TILES - 1):
                            if isinstance(c, int) and c == 0 and k % 4 == 0:
                                pe.wait_ge(hp_done, l * UNITS + k // 4 + 1)
                            products(k, False)
                        if isinstance(c, int) and c == 0:
                            pe.wait_ge(hp_done, (l + 1) * UNITS)
                        with pe.If(general > 0):
                            for k in range(NODE_TILES):
                                pe.wait_ge(rest_loaded, (n * NODE_TILES + k + 1) * 16)
                                for s in range(PIECES):
                                    last = nc.tensor.matmul(agg_ps[b][:, 0:CW], hp[:, k, s, :], rest_view(c),
                                                            start=False, stop=False)
                                last.then_inc(rest_free, 1)
                            products(NODE_TILES - 1, True).then_inc(agg_done, 1)
                        with pe.Else():
                            products(NODE_TILES - 1, True).then_inc(agg_done, 1)

                    def hidden(l, c, b):
                        if isinstance(c, int) and c == 0:
                            pe.wait_ge(m_done, l + 1)
                            pe.wait_ge(w1_scaled, l + 1)
                        if not (isinstance(c, int) and c < 2):
                            pe.wait_ge(h1_ev, l * CHUNKS + c - 1)
                        for h in range(2):
                            nc.tensor.matmul(w1_ps[b][h][:, 0:CW], m6[:, h * P:(h + 1) * P], s6[:, ds(c * CW, CW)],
                                             start=True, stop=False)
                        if later(l):
                            pe.wait_ge(agg_ev, (l - 1) * CHUNKS + c + 1)
                        sums_in = aggT[:, 0:CW] if later(l) else agg0[:, c * CW:(c + 1) * CW]
                        for h in range(2):
                            nc.tensor.matmul(w1_ps[b][h][:, 0:CW], wp[:, W1A + h * P:W1A + (h + 1) * P], sums_in,
                                             start=False, stop=True).then_inc(w1_done, 1)

                    def edge_weights(l):
                        pe.wait_ge(l_mp, (l + 1) * 16)
                        nc.tensor.matmul(w2_ps[0][0:SK, 0:HID], mp[:, EWB:EWB + SK], mp[:, W1B:W1B + HID],
                                         start=True, stop=True).then_inc(m_ps, 1)

                    def bounds(l):
                        pe.wait_ge(uw_done, l + 1)
                        for h in range(2):
                            last = nc.tensor.matmul(w2_ps[1][:, 0:D], ones[:, :], uw[:, h * P:(h + 1) * P],
                                                    start=(h == 0), stop=(h == 1))
                        last.then_inc(bound, 1)

                    def project(l, u, final):
                        if u == 0 and not final:
                            pe.wait_ge(w2_scaled, l + 1)
                        pe.wait_ge(relu_done, l * UNITS + u + 1)
                        if u == 0:
                            pe.wait_ge(relu0_done, l + 1)
                        if u >= 2:
                            pe.wait_ge(t_done, l * UNITS + u - 1)
                        r = rows_of(u)
                        for j in range(tiles_of(u)):
                            for h in range(2):
                                a = u * UW + j * P
                                last = nc.tensor.matmul(w2_ps[u % 2][0:r, j * P:(j + 1) * P], h1[:, h, a:a + r],
                                                        wp[:, W2T + h * P:W2T + (h + 1) * P], start=(h == 0), stop=(h == 1))
                        last.then_inc(w2_done, 1)

                    def layer(l, final):
                        aggregate(l, 0, 0)
                        edge_weights(l)
                        aggregate(l, 1, 1)
                        hidden(l, 0, 0)
                        aggregate(l, 2, 0)
                        hidden(l, 1, 1)
                        if not final:
                            bounds(l)
                        with pe.Fori(1, CHUNKS // 2) as i:
                            aggregate(l, 2 * i + 1, 1)
                            hidden(l, 2 * i, 0)
                            aggregate(l, 2 * i + 2, 0)
                            hidden(l, 2 * i + 1, 1)
                        hidden(l, CHUNKS - 1, 0)
                        for u in range(UNITS):
                            project(l, u, final)

                    pe.wait_ge(ones_done, 1)
                    pe.sem_inc(rest_free, 1)
                    edge_weights(0)
                    for c in range(CHUNKS):
                        hidden(0, c, c % 2)
                        if c == 1:
                            bounds(0)
                    for u in range(UNITS):
                        project(0, u, False)
                    with pe.Fori(1, LAYERS - 1) as l:
                        layer(l, False)
                    layer(LAYERS - 1, True)

                @block.scalar
                def _(act):
                    def evac_agg(l, c, b):
                        n = (l - 1) * CHUNKS + c
                        act.wait_ge(agg_done, n + 1)
                        if not (isinstance(c, int) and c == 0):
                            act.wait_ge(w1_done, (l * CHUNKS + c) * 2)
                        nc.scalar.activation(aggT[:, 0:CW], agg_ps[b][:, 0:CW], ACT.Copy).then_inc(agg_ev, 1)

                    def evac_h1(l, c, b):
                        for h in range(2):
                            if isinstance(c, int) and c == CHUNKS - 1 and h == 1:
                                act.wait_ge(st_last, l + 1)
                            else:
                                act.wait_ge(st_done, l * (2 * CHUNKS - 1) + 2 * c + h + 1)
                            last = nc.scalar.activation(h1[:, h, ds(c * CW, CW)], w1_ps[b][h][:, 0:CW], ACT.Identity,
                                                        bias=wp[:, B1 + h:B1 + h + 1])
                        last.then_inc(h1_ev, 1)

                    def relu(l, u):
                        for h in range(1 if u == 0 else 2):
                            v = h1[:, h, u * UW:min((u + 1) * UW, COLS)]
                            last = nc.scalar.activation(v, v, ACT.Relu, bias=shift[:, h:h + 1], scale=scale[:, h:h + 1])
                        last.then_inc(relu_done, 1)

                    def normalise(l, final):
                        act.wait_ge(mv_done, l + 1)
                        nc.scalar.activation(sd[:, :], mv[:, :, 1], ACT.Sqrt, bias=cst[:, EPSC:EPSC + 1]).then_inc(sd_done, 1)
                        act.wait_ge(bn_ready, l + 1)
                        for u in range(UNITS + 2):
                            if u < UNITS:
                                relu(l, u)
                            if u >= 2 and not final:
                                act.wait_ge(t_done, l * UNITS + u - 1)
                                nc.scalar.activation(hp_view(u - 2, 0), unit_view(0, u - 2), ACT.Relu).then_inc(hi_done, 1)

                    def layer(l, final):
                        act.wait_ge(l_wp, (l + 1) * 16)
                        evac_agg(l, 0, 0)
                        with act.Fori(0, CHUNKS // 2) as i:
                            evac_agg(l, 2 * i + 1, 1)
                            evac_h1(l, 2 * i, 0)
                            evac_agg(l, 2 * i + 2, 0)
                            evac_h1(l, 2 * i + 1, 1)
                        evac_h1(l, CHUNKS - 1, 0)
                        normalise(l, final)

                    for c in range(CHUNKS):
                        evac_h1(0, c, c % 2)
                    normalise(0, False)
                    with act.Fori(1, LAYERS - 1) as l:
                        layer(l, False)
                    layer(LAYERS - 1, True)

                @block.gpsimd
                def _(pool):
                    nc.gpsimd.memset(ones[:, :], 1.0).then_inc(ones_done, 1)

                @block.vector
                def _(dve):
                    V = nc.vector

                    def absolute(out, v):
                        return V.scalar_tensor_tensor(out, v, -1.0, v, ALU.mult, ALU.max)

                    def weights(l, final):
                        steps = Steps(dve, w_chain, l * WSTEPS)
                        dve.wait_ge(l_wp, (l + 1) * 16)
                        w1 = wp[:, W1A:W1A + HID]
                        w2 = wp[:, W2T:W2T + HID].rearrange("p (h f) -> p h f", h=2)
                        if later(l):
                            V.tensor_scalar(w1, w1, inv[:, 0:1], None, ALU.mult).then_inc(w1_scaled, 1)
                        else:
                            V.tensor_scalar(w1, w1, 1.0 / LN_SCALE, None, ALU.mult).then_inc(w1_scaled, 1)
                        dve.wait_ge(m_ps, l + 1)
                        steps.then(V.tensor_copy(m6[:, :], w2_ps[0][0:SK, 0:HID]))
                        steps.then(V.scalar_tensor_tensor(mt[:, :], m6[:, :], cst[0:SK, M_A:M_A + 1], w2_ps[0][0:SK, 0:HID],
                                                          ALU.mult, ALU.add))
                        steps.then(V.tensor_copy(m6[:, :], mt[:, :]))
                        steps.then(V.scalar_tensor_tensor(mt[:, :], m6[:, :], cst[0:SK, M_B:M_B + 1], mt[:, :], ALU.mult, ALU.add))
                        V.tensor_copy(m6[:, :], mt[:, :]).then_inc(m_done, 1)
                        if final:
                            return steps
                        steps.then(absolute(ab, wp[:, BNW:BNB + 2]))
                        steps.then(V.scalar_tensor_tensor(ub, ab[:, 0:2], float(N_NODES) ** 0.5, ab[:, 2:4], ALU.mult,
                                                          ALU.add))
                        parts = uw[:, :].rearrange("p (h f) -> p h f", h=2)
                        steps.then(absolute(parts, w2))
                        V.tensor_tensor(parts, parts, ub.unsqueeze(2).to_broadcast([P, 2, D]), ALU.mult).then_inc(uw_done, 1)
                        return steps

                    def scale_of_bound(l, steps):
                        b2 = wp[:, B2:B2 + D]
                        steps.then(absolute(row[:, 0, :], b2))
                        dve.wait_ge(bound, l + 1)
                        steps.then(V.scalar_tensor_tensor(row[:, 1, :], row[:, 0, :], 1e-30, w2_ps[1][:, 0:D], ALU.max,
                                                          ALU.add))
                        steps.then(V.tensor_scalar(row[:, 2, :].bitcast(I32), row[:, 1, :].bitcast(I32), 0x7F800000, None,
                                                   ALU.bitwise_and))
                        steps.then(V.reciprocal(row[:, 3, :], row[:, 2, :]))

                    def scale_weights(l, steps):
                        b2 = wp[:, B2:B2 + D]
                        w2 = wp[:, W2T:W2T + HID].rearrange("p (h f) -> p h f", h=2)
                        steps.then(V.tensor_scalar(row[:, 0, :], row[:, 3, :], TOP, None, ALU.mult))
                        steps.then(V.tensor_tensor(b2, b2, row[:, 0, :], ALU.mult))
                        steps.then(V.tensor_tensor(w2, w2, row[:, 0:1, :].to_broadcast([P, 2, D]), ALU.mult))

                    def scale_back(l, steps):
                        steps.then(V.tensor_scalar(row[:, 3, :], row[:, 2, :], 1.0 / TOP, None, ALU.mult))
                        steps.then(V.tensor_tensor(row[:, 1, :], row[:, 3, :], ident[:, :], ALU.mult))
                        V.tensor_reduce(inv[:, 0:1], row[:, 1, :], AX.X, ALU.add).then_inc(w2_scaled, 1)

                    def statistics(l, c, b, last=False):
                        cols = N_NODES - (CHUNKS - 1) * CW if last else CW
                        for h in range(2):
                            dve.wait_ge(w1_done, (l * CHUNKS + c) * 2 + h + 1)
                            V.bn_stats(stats[:, h, ds(c * 6, 6)], w1_ps[b][h][:, 0:cols]
                                       ).then_inc(st_last if last and h == 1 else st_done, 1)

                    def bn(l):
                        statistics(l, CHUNKS - 1, 0, True)
                        steps = Steps(dve, bn_c, l * BN_STEPS)
                        dve.wait_ge(l_c, 16)
                        dve.wait_ge(st_last, l + 1)
                        for h in range(2):
                            last = V.bn_aggr(mv[:, h, :], stats[:, h, :])
                        last.then_inc(mv_done, 1)
                        dve.wait_ge(sd_done, l + 1)
                        V.tensor_tensor(mean_b, mv[:, :, 0], wp[:, B1:B1 + 2], ALU.add)
                        steps.then(V.reciprocal(rstd, sd))
                        steps.then(V.tensor_tensor(scale, rstd, wp[:, BNW:BNW + 2], ALU.mult))
                        steps.then(V.tensor_tensor(ms, mean_b, scale, ALU.mult))
                        V.tensor_tensor(shift, wp[:, BNB:BNB + 2], ms, ALU.subtract).then_inc(bn_ready, 1)
                        v = h1[:, 1, 0:UW]
                        dve.wait_ge(h1_ev, (l + 1) * CHUNKS)
                        dve.wait_ge(bn_ready, l + 1)
                        steps.then(V.tensor_scalar(v, v, scale[:, 1:2], shift[:, 1:2], ALU.mult, ALU.add))
                        V.tensor_scalar(v, v, 0.0, None, ALU.max).then_inc(relu0_done, 1)
                        assert steps.n == BN_STEPS

                    def add_bias(l, u):
                        k, r = tiles_of(u), rows_of(u)
                        dve.wait_ge(w2_done, l * UNITS + u + 1)
                        V.tensor_tensor(unit_view(0, u), w2_view(u),
                                        wp[0:r, B2:B2 + D].unsqueeze(1).to_broadcast([r, k, D]), ALU.add).then_inc(t_done, 1)

                    def low_piece(l, u):
                        dve.wait_ge(hi_done, l * UNITS + u + 1)
                        V.scalar_tensor_tensor(hp_view(u, 1), unit_view(0, u), 0.0, hp_view(u, 0), ALU.max,
                                               ALU.subtract).then_inc(hp_done, 1)

                    def residual(l, u):
                        k, r = tiles_of(u), rows_of(u)
                        dve.wait_ge(t_done, l * UNITS + u + 1)
                        V.tensor_tensor(unit_view(1, u), unit_view(0, u), x_res[0:r, 4 * u:4 * u + k, :],
                                        ALU.add).then_inc(o_done, 1)

                    def layer(l, final):
                        steps = weights(l, final)
                        parts = {1: scale_of_bound, 2: scale_weights, 3: scale_back}
                        for c in range(CHUNKS - 1):
                            statistics(l, c, c % 2)
                            if c in parts and not final:
                                parts[c](l, steps)
                        assert final or steps.n == WSTEPS
                        bn(l)
                        if final:
                            dve.wait_ge(l_x, 32)
                        for u in range(UNITS + 1):
                            if u < UNITS:
                                add_bias(l, u)
                            if u >= 1:
                                residual(l, u - 1) if final else low_piece(l, u - 1)
                    layer(0, False)
                    with dve.Fori(1, LAYERS - 1) as l:
                        layer(l, False)
                    layer(LAYERS - 1, True)


def kernel(x, src, dst, edge_attr_16, L0_gnn_W1, L0_gnn_B1, L0_gnn_BNW, L0_gnn_BNB, L0_gnn_W2, L0_gnn_B2,
           L0_gnn_EW, L0_gnn_EB):
    import numpy as np
    import concourse.bacc as bacc
    from concourse.bass_utils import run_bass_kernel_spmd

    def by_tile(a, fill, own=None):
        a = np.asarray(a)
        pad = np.full((PAD_TILES * P,) + a.shape[1:], fill, a.dtype)
        pad[:N_EDGES] = a
        if own is not None:
            pad[SELF_TILE * P:SELF_TILE * P + N_NODES] = own
        return np.ascontiguousarray(np.moveaxis(pad.reshape((PAD_TILES, P) + a.shape[1:]), 1, 0))

    rec = np.ones((N_EDGES, REC), np.float32)
    rec[:, 1:] = np.asarray(edge_attr_16)
    attr = by_tile(rec, 0).reshape(P, PAD_TILES * REC)

    w1, w2 = np.asarray(L0_gnn_W1), np.asarray(L0_gnn_W2)
    ew, eb = np.asarray(L0_gnn_EW), np.asarray(L0_gnn_EB)
    wpack = np.zeros((LAYERS, P, WP_COLS), np.float32)
    wpack[:, :, W1A:W1A + HID] = w1[:, :, :D].transpose(0, 2, 1)
    wpack[:, :, W2T:W2T + HID] = w2.transpose(0, 2, 1).reshape(LAYERS, 2, P, D).transpose(0, 2, 1, 3).reshape(LAYERS, P, HID)
    for at, v in ((B1, L0_gnn_B1), (BNW, L0_gnn_BNW), (BNB, L0_gnn_BNB)):
        wpack[:, :, at:at + 2] = np.asarray(v).reshape(LAYERS, 2, P).transpose(0, 2, 1)
    wpack[:, :, B2:B2 + D] = np.asarray(L0_gnn_B2)[:, None, :]
    mpack = np.zeros((LAYERS, P, MP_COLS), np.float32)
    mpack[:, :, W1B:W1B + HID] = w1[:, :, D:].transpose(0, 2, 1)
    for t in range(TERMS):
        mpack[:, :, EWB + t * REC] = eb
        mpack[:, :, EWB + t * REC + 1:EWB + (t + 1) * REC] = ew
    consts = np.zeros((P, C_COLS), np.float32)
    for t, (s_piece, m_piece) in enumerate(((0, 0), (0, 1), (0, 2), (1, 0), (1, 1), (2, 0))):
        rows = slice(t * REC, (t + 1) * REC)
        consts[t * REC, PLUS1] = 1.0
        consts[rows, S_A] = -1.0 if s_piece >= 1 else 0.0
        consts[rows, S_B] = -1.0 if s_piece >= 2 else 0.0
        consts[rows, M_A] = -1.0 if m_piece >= 1 else 0.0
        consts[rows, M_B] = -1.0 if m_piece >= 2 else 0.0
        consts[0:REC, STACK + t * REC:STACK + (t + 1) * REC] = np.eye(REC)
    consts[:, EPSC] = EPS

    arrays = {
        "x": np.ascontiguousarray(x), "src": by_tile(src, 0, np.arange(N_NODES)),
        "dst": by_tile(dst, -1, np.arange(N_NODES)), "attr": attr, "consts": consts, "wpack": wpack, "mpack": mpack,
    }
    nc = bacc.Bacc("TRN2", target_bir_lowering=False, num_devices=1)
    ins = [nc.dram_tensor(n, a.shape, mybir.dt.from_np(a.dtype), kind="ExternalInput").ap() for n, a in arrays.items()]
    out = nc.dram_tensor("out", (N_NODES, D), F32, kind="ExternalOutput").ap()

    def scratch(name, shape, dt):
        return nc.dram_tensor(name, shape, dt, kind="Internal").ap()
    gin_program(nc, *ins, out, scratch("keys_dram", (P, PAD_TILES * KREC), F32), scratch("window_dram", (P,), I32), scratch("rest_dram", (P, NODE_TILES * COLS), BF16))
    r = run_bass_kernel_spmd(nc, [arrays], core_ids=[0])
    return r.results[0]["out"]
```
